# Optimizing a Trainium2 kernel written in Bass

```python
import numpy as np
import jax
import jax.numpy as jnp

def _softmax(x, axis=-1):
    return jax.nn.softmax(x, axis=axis)

def _gelu(x):
    return jax.nn.gelu(x, approximate=True)

def _silu(x):
    return jax.nn.silu(x)

def _sigmoid(x):
    return jax.nn.sigmoid(x)

def _layernorm(x, axis=-1, eps=1e-05):
    m = jnp.mean(x, axis=axis, keepdims=True)
    v = jnp.var(x, axis=axis, keepdims=True)
    return (x - m) / jnp.sqrt(v + eps)

def _scatter_add(tgt, idx, src, axis=0):
    return tgt.at[idx].add(src)

def _segment_sum(src, seg, n):
    return jax.ops.segment_sum(src, seg, n)
kernel_name = 'mk_xattn_seq_d2_seqx_r4_6c12bf'

def setup_inputs(seed: int=0):
    np.random.seed(seed)
    _w = jnp.asarray

    def _rec_inputs():
        import jax
        import jax.numpy as jnp
        _rk = jax.random.key(seed)
        x = -0.000125 + 0.9999 * jax.random.normal(jax.random.fold_in(_rk, 1), (16, 128, 1024), jnp.float32)
        _lenS = 128 - jax.random.randint(jax.random.fold_in(_rk, 7), (16,), 0, max(1, 128 // 4) + 1, jnp.int32)
        _lenS2 = 128 - jax.random.randint(jax.random.fold_in(_rk, 8), (16,), 0, max(1, 128 // 4) + 1, jnp.int32)
        _ctx_4096P = jax.random.normal(jax.random.fold_in(_rk, 11), (16, 16, 1024), jnp.float32)
        _ctx_4096c = jax.random.dirichlet(jax.random.fold_in(_rk, 511), 0.3 * jnp.ones((16,), jnp.float32), (16, 128))
        _ctx_4096t = jnp.einsum('bsk,bkd->bsd', _ctx_4096c, _ctx_4096P)
        _ctx_4096t = _ctx_4096t * jax.lax.rsqrt(jnp.mean(jnp.square(_ctx_4096t)) + 1e-12) * 0.953939
        ctx_4096 = -1.52775e-05 + 0.999936 * (_ctx_4096t + 0.3 * jax.random.normal(jax.random.fold_in(_rk, 611), (16, 128, 1024), jnp.float32))
        _validS = jnp.arange(128)[None, :] < _lenS[:, None]
        _validS2 = jnp.arange(128)[None, :] < _lenS2[:, None]
        _causal = jnp.tril(jnp.ones((128, 128), dtype=bool))
        mask_Bx1x4096_ff1 = jnp.where(jnp.ones((16, 1, 1024), dtype=bool), 1.0, 0.0).astype(jnp.float32)
        return (x, ctx_4096, mask_Bx1x4096_ff1)
    x, ctx_4096, mask_Bx1x4096_ff1 = _rec_inputs()

    def _L0_xattn_setup():
        import jax, jax.numpy as jnp
        import numpy as np
        B, C, N, H = (16, 128, 1024, 8)
        key = jax.random.key(seed)
        ks = jax.random.split(key, 10)
        s = 0.02
        return {'rgb_emb': jax.random.normal(ks[0], (B, C, N), jnp.float32), 'geo_emb': jax.random.normal(ks[1], (B, C, N), jnp.float32), 'wq_rgb': jax.random.normal(ks[2], (C, C), jnp.float32) * s, 'wk_rgb': jax.random.normal(ks[3], (C, C), jnp.float32) * s, 'wv_rgb': jax.random.normal(ks[4], (C, C), jnp.float32) * s, 'wq_point': jax.random.normal(ks[5], (C, C), jnp.float32) * s, 'wk_point': jax.random.normal(ks[6], (C, C), jnp.float32) * s, 'wv_point': jax.random.normal(ks[7], (C, C), jnp.float32) * s, 'proj_r2p': jax.random.normal(ks[8], (C, C), jnp.float32) * s, 'proj_p2r': jax.random.normal(ks[9], (C, C), jnp.float32) * s}
    _L0_xattn_all = _L0_xattn_setup()
    _L0_xattn_in = {k: v for k, v in _L0_xattn_all.items() if k in ('wq_rgb', 'wk_rgb', 'wv_rgb', 'wq_point', 'wk_point', 'wv_point', 'proj_r2p', 'proj_p2r')}
    del _L0_xattn_all

    def _L1_xattn_setup():
        import jax, jax.numpy as jnp
        import numpy as np
        NUM_HEADS = 8
        CHUNK = 64
        EPS = 1e-05
        NEG = -1000000000.0

        def _chunk_attn(q, k, v, masks, W_in, b_in, W_out, b_out):
            N, C, T = q.shape
            H, Dh = (NUM_HEADS, C // NUM_HEADS)
            nc = T // CHUNK
            Wq, Wk, Wv = jnp.split(W_in, 3, axis=0)
            bq, bk, bv = jnp.split(b_in, 3, axis=0)

            def proj(t, W, b):
                t = t.transpose(0, 2, 1) @ W.T + b
                return t.reshape(N, nc, CHUNK, H, Dh)
            qh = proj(q, Wq, bq)
            kh = proj(k, Wk, bk)
            vh = proj(v, Wv, bv)
            scale = 1.0 / jnp.sqrt(jnp.asarray(Dh, q.dtype))
            scores = jnp.einsum('bnqhd,bnkhd->bnhqk', qh, kh) * scale
            km = masks[:, 0, :].reshape(N, nc, CHUNK)
            scores = scores + jnp.where(km[:, :, None, None, :] > 0, 0.0, NEG)
            attn = jax.nn.softmax(scores, axis=-1)
            out = jnp.einsum('bnhqk,bnkhd->bnqhd', attn, vh).reshape(N, T, C)
            out = out @ W_out.T + b_out
            out = out.transpose(0, 2, 1) * masks
            return out
        key = jax.random.key(seed)
        ks = jax.random.split(key, 8)
        N, C, T = (4, 128, 1024)
        x = jax.random.normal(ks[0], (N, C, T), dtype=jnp.float32)
        q = jax.random.normal(ks[1], (N, C, T), dtype=jnp.float32)
        k = jax.random.normal(ks[2], (N, C, T), dtype=jnp.float32)
        v = jax.random.normal(ks[3], (N, C, T), dtype=jnp.float32)
        masks = jnp.ones((N, 1, T), dtype=jnp.float32)
        s = 1.0 / np.sqrt(C)
        W_in = jax.random.normal(ks[4], (3 * C, C), dtype=jnp.float32) * s
        b_in = jnp.zeros((3 * C,), dtype=jnp.float32)
        W_out = jax.random.normal(ks[5], (C, C), dtype=jnp.float32) * s
        b_out = jnp.zeros((C,), dtype=jnp.float32)
        return {'x': x, 'q': q, 'k': k, 'v': v, 'masks': masks, 'W_in': W_in, 'b_in': b_in, 'W_out': W_out, 'b_out': b_out}
    _L1_xattn_all = _L1_xattn_setup()
    _L1_xattn_in = {k: v for k, v in _L1_xattn_all.items() if k in ('W_in', 'b_in', 'W_out', 'b_out')}
    del _L1_xattn_all
    return {'x': x, 'ctx_4096': ctx_4096, 'mask_Bx1x4096_ff1': mask_Bx1x4096_ff1, 'L0_xattn_wq_rgb': _L0_xattn_in['wq_rgb'], 'L0_xattn_wk_rgb': _L0_xattn_in['wk_rgb'], 'L0_xattn_wv_rgb': _L0_xattn_in['wv_rgb'], 'L0_xattn_wq_point': _L0_xattn_in['wq_point'], 'L0_xattn_wk_point': _L0_xattn_in['wk_point'], 'L0_xattn_wv_point': _L0_xattn_in['wv_point'], 'L0_xattn_proj_r2p': _L0_xattn_in['proj_r2p'], 'L0_xattn_proj_p2r': _L0_xattn_in['proj_p2r'], 'L1_xattn_W_in': _L1_xattn_in['W_in'], 'L1_xattn_b_in': _L1_xattn_in['b_in'], 'L1_xattn_W_out': _L1_xattn_in['W_out'], 'L1_xattn_b_out': _L1_xattn_in['b_out']}

def reference(x, ctx_4096, mask_Bx1x4096_ff1, L0_xattn_wq_rgb, L0_xattn_wk_rgb, L0_xattn_wv_rgb, L0_xattn_wq_point, L0_xattn_wk_point, L0_xattn_wv_point, L0_xattn_proj_r2p, L0_xattn_proj_p2r, L1_xattn_W_in, L1_xattn_b_in, L1_xattn_W_out, L1_xattn_b_out):
    import jax
    import jax.numpy as jnp

    def _L0_xattn_ref(rgb_emb, geo_emb, wq_rgb, wk_rgb, wv_rgb, wq_point, wk_point, wv_point, proj_r2p, proj_p2r):
        import jax, jax.numpy as jnp
        import numpy as np
        B, C, N, H = (16, 128, 1024, 8)
        rgb = jnp.transpose(rgb_emb, (0, 2, 1))
        geo = jnp.transpose(geo_emb, (0, 2, 1))
        b, n, c = rgb.shape
        d = c // H
        scale = d ** (-0.5)

        def heads(x, w):
            return (x @ w.T).reshape(b, n, H, d).transpose(0, 2, 1, 3)

        def xca(q, k, v):
            attn = jax.nn.softmax(jnp.einsum('bhni,bhnj->bhij', q, k) * scale, axis=-1)
            out = jnp.einsum('bhnd,bhde->bhne', v, attn)
            return out.transpose(0, 2, 1, 3).reshape(b, n, c)
        res_p2r = xca(heads(rgb, wq_rgb), heads(geo, wk_point), heads(geo, wv_point)) @ proj_p2r.T
        res_r2p = xca(heads(geo, wq_point), heads(rgb, wk_rgb), heads(rgb, wv_rgb)) @ proj_r2p.T
        rgb_att = jnp.transpose(rgb + res_p2r, (0, 2, 1))
        geo_att = jnp.transpose(geo + res_r2p, (0, 2, 1))
        return rgb_att + geo_att

    def _L1_xattn_ref(x, q, k, v, masks, W_in, b_in, W_out, b_out):
        import jax, jax.numpy as jnp
        import numpy as np
        NUM_HEADS = 8
        CHUNK = 64
        EPS = 1e-05
        NEG = -1000000000.0

        def _chunk_attn(q, k, v, masks, W_in, b_in, W_out, b_out):
            N, C, T = q.shape
            H, Dh = (NUM_HEADS, C // NUM_HEADS)
            nc = T // CHUNK
            Wq, Wk, Wv = jnp.split(W_in, 3, axis=0)
            bq, bk, bv = jnp.split(b_in, 3, axis=0)

            def proj(t, W, b):
                t = t.transpose(0, 2, 1) @ W.T + b
                return t.reshape(N, nc, CHUNK, H, Dh)
            qh = proj(q, Wq, bq)
            kh = proj(k, Wk, bk)
            vh = proj(v, Wv, bv)
            scale = 1.0 / jnp.sqrt(jnp.asarray(Dh, q.dtype))
            scores = jnp.einsum('bnqhd,bnkhd->bnhqk', qh, kh) * scale
            km = masks[:, 0, :].reshape(N, nc, CHUNK)
            scores = scores + jnp.where(km[:, :, None, None, :] > 0, 0.0, NEG)
            attn = jax.nn.softmax(scores, axis=-1)
            out = jnp.einsum('bnhqk,bnkhd->bnqhd', attn, vh).reshape(N, T, C)
            out = out @ W_out.T + b_out
            out = out.transpose(0, 2, 1) * masks
            return out
        out = _chunk_attn(q, k, v, masks, W_in, b_in, W_out, b_out) + x
        mu = jnp.mean(out, axis=2, keepdims=True)
        var = jnp.mean(jnp.square(out - mu), axis=2, keepdims=True)
        return (out - mu) * jax.lax.rsqrt(var + EPS)
    x = _L0_xattn_ref(x, ctx_4096, L0_xattn_wq_rgb, L0_xattn_wk_rgb, L0_xattn_wv_rgb, L0_xattn_wq_point, L0_xattn_wk_point, L0_xattn_wv_point, L0_xattn_proj_r2p, L0_xattn_proj_p2r)
    x = _L1_xattn_ref(x, ctx_4096, ctx_4096, ctx_4096, mask_Bx1x4096_ff1, L1_xattn_W_in, L1_xattn_b_in, L1_xattn_W_out, L1_xattn_b_out)
    return x

_drawn_inputs = setup_inputs


def setup_inputs(seed=0):
    import zlib

    import numpy as np

    out = dict(_drawn_inputs(seed))
    spreads = {'L1_xattn_b_in': (0.0, 0.572), 'L1_xattn_b_out': (0.0, 0.8)}
    factors = {'L0_xattn_wq_rgb': 8.0,
     'L0_xattn_wk_rgb': 8.0,
     'L0_xattn_wv_rgb': 5.906,
     'L0_xattn_wq_point': 8.0,
     'L0_xattn_wk_point': 8.0,
     'L0_xattn_wv_point': 6.357,
     'L0_xattn_proj_r2p': 5.729,
     'L0_xattn_proj_p2r': 6.144}
    for name, (base, spread) in spreads.items():
        noise = np.random.default_rng([zlib.crc32(name.encode()), seed]).standard_normal(out[name].shape)
        drawn = base * np.exp(spread * noise) if base else spread * noise
        out[name] = jnp.asarray(drawn.astype(out[name].dtype))
    for name, factor in factors.items():
        out[name] = (out[name] * factor).astype(out[name].dtype)
    return out
```

```python
from contextlib import ExitStack

import concourse.bass as bass
from concourse import mybir

B, C, T, H = 16, 128, 1024, 8
D = C // H
CH = 64
PR = 2 * CH
NP = T // PR
HALF = T // 2
SCALE = float(D) ** -0.5
NEG = -1.0e9
PTS = 2
OFF = -1.0e30
EPS = 1e-5

F32 = mybir.dt.float32
BF16 = mybir.dt.bfloat16
ALU = mybir.AluOpType
ACT = mybir.ActivationFunctionType
AX_X = mybir.AxisListType.X

TAIL = ["wo0", "wo1"]
FRONT = ["M", "A", "k0", "S", "k1", "V0", "QA", "V1", "PM", "y0", "y1", "q0", "q1"]
PLACE = {0: ["M"], 1: ["A", "k0"], 2: ["S", "k1"], 3: ["V0", "QA"], 4: ["V1", "PM"],
         5: ["y0", "y1"], 6: ["q0", "q1"], 7: []}
USES = len(TAIL) + len(FRONT)


def program(nc, x, g, xT, gT, mask, mask_ck, w_l0, w_v, w_qkv, wo, b_col, b_v, consts,
            indicator, out):
    with ExitStack() as ctx:
        def sb(name, shape, dt=F32):
            return ctx.enter_context(nc.sbuf_tensor(name, shape, dt))

        def ps(name):
            return ctx.enter_context(nc.psum_tensor(name, [C, HALF], F32))

        def sem(name):
            return ctx.enter_context(nc.semaphore(name))

        X = sb("X", [C, 2, T])
        G = sb("G", [C, 2, T])
        XT = sb("XT", [C, T])
        GT = sb("GT", [C, T])
        mrow = sb("mrow", [2, NP, CH])
        WL0 = sb("WL0", [C, 6, C])
        WV = sb("WV", [C, 2, C])
        WQKV = sb("WQKV", [C, 3, C])
        WOZ = sb("WOZ", [C, 4, C])
        bcol = sb("bcol", [C, 4])
        bv = sb("bv", [C, C])
        ident = sb("ident", [C, C])
        onesbd = sb("onesbd", [C, 2, D])
        offb = sb("offb", [C, C])
        i2b = sb("i2b", [C, CH], BF16)
        indb = sb("indb", [2, C], BF16)
        nb = sb("nb", [C, B * NP])
        halfneg = sb("halfneg", [C, 1])
        epsc = sb("epsc", [C, 1])
        carrier = sb("carrier", [C, 1])
        Msb = sb("Msb", [C, C])
        Asb = sb("Asb", [C, 2, C])
        Ssb = sb("Ssb", [C, 2, C])
        nmx0 = sb("nmx0", [C, 2])
        E0 = sb("E0", [C, 2, C])
        sum0 = sb("sum0", [C, 2])
        rs0 = sb("rs0", [C, 2])
        ET = sb("ET", [C, 2, C])
        QAsb = sb("QAsb", [C, 2, C])
        WY = sb("WY", [C, 2, C])
        Y = sb("Y", [C, 2, T])
        qs = sb("qs", [C, T])
        qb = sb("qb", [C, 2, T], BF16)
        ks = sb("ks", [C, 2, T])
        kb = sb("kb", [C, T], BF16)
        Qz0, Qz1 = sb("Qz0", [C, H, T]), sb("Qz1", [C, H, T])
        Kz0, Kz1 = sb("Kz0", [C, H, T], BF16), sb("Kz1", [C, H, T], BF16)
        Qz, Kz = [Qz0, Qz1], [Kz0, Kz1]
        Vz = sb("Vz", [C, 2, NP, H, 2, D])
        mbias = sb("mbias", [2, 2, NP, CH], BF16)
        nmx = sb("nmx", [C, 2, H], BF16)
        mex = sb("mex", [C, 2, H, CH], BF16)
        bones = sb("bones", [C, 2, CH], BF16)
        PT = sb("PT", [C, PTS, HALF])
        rden = sb("rden", [C, HALF])
        On = sb("On", [C, 2, NP, 2, CH])
        R = sb("R", [C, T])
        maskb = sb("maskb", [C, T])
        stats = sb("stats", [C, 2, 6])
        mv = sb("mv", [C, 2])
        ve = sb("ve", [C, 1])
        rstd = sb("rstd", [C, 1])

        misc = [ps("misc0"), ps("misc1")]
        MX = [ps("mx0"), ps("mx1")]
        SC = [ps("sc0"), ps("sc1")]
        PVb, DN = ps("pv"), ps("dn")

        consts_in = sem("consts_in")
        setup = sem("setup")
        setup_pool = sem("setup_pool")
        setup_act = sem("setup_act")
        zeroed_pool, zeroed_dve = sem("zeroed_pool"), sem("zeroed_dve")
        maskb_in = sem("maskb_in")
        turned_in = sem("turned_in")
        loaded = [sem("loaded0"), sem("loaded1")]
        misc_ready = [sem("misc_ready0"), sem("misc_ready1")]
        misc_out = [sem("misc_out0"), sem("misc_out1")]
        l0_max, l0_exp, l0_turned = sem("l0_max"), sem("l0_exp"), sem("l0_turned")
        cast_k, cast_q = sem("cast_k"), sem("cast_q")
        q_spread = [sem("q_spread0"), sem("q_spread1")]
        k_spread = [sem("k_spread0"), sem("k_spread1")]
        mbias_ready = sem("mbias_ready")
        mx_ready, mx_taken, m_ready = sem("mx_ready"), sem("mx_taken"), sem("m_ready")
        sc_ready, exp_done = sem("sc_ready"), sem("exp_done")
        pv_done = sem("pv_done")
        rden_done, norm_done = sem("rden_done"), sem("norm_done")
        added = sem("added")
        stats_done, aggr_done, ve_done, rstd_done = sem("stats_done"), sem("aggr_done"), sem("ve_done"), sem("rstd_done")
        normed = sem("normed")
        stored = sem("stored")

        NCONST = 11 + 16

        class At:
            def __init__(self, i, par):
                self.i, self.par = i, par

            def b(self, shift=0):
                return self.i * 2 + (self.par + shift)

            def first(self, shift=0):
                return isinstance(self.i, int) and self.b(shift) < 0

        def past(eng, s, at, per, shift, extra):
            if isinstance(at.i, int) and per * at.b(shift) + extra <= 0:
                return
            eng.wait_ge(s, at.i * (2 * per) + (per * (at.par + shift) + extra))

        def use(at, name):
            if at is None:
                n = FRONT.index(name)
                return n % 2, n // 2, 0
            n = USES * (at.par + 1) - 4 + (TAIL + FRONT).index(name)
            if at is LAST:
                n -= len(FRONT)
            return n % 2, n // 2, at.i * USES

        def wait_use(eng, sems, at, name, back):
            bank, turn, base = use(at, name)
            if isinstance(base, int) and base + turn + back <= 0:
                return
            eng.wait_ge(sems[bank], base + (turn + back))

        def take(eng, at, name):
            wait_use(eng, misc_ready, at, name, 1)
            return misc[use(at, name)[0]]

        def put(eng, at, name):
            wait_use(eng, misc_out, at, name, 0)
            return misc[use(at, name)[0]]

        def evicted(eng, at, name):
            wait_use(eng, misc_out, at, name, 1)

        def out_sem(at, name):
            return misc_out[use(at, name)[0]]

        def ready_sem(at, name):
            return misc_ready[use(at, name)[0]]

        START = At(-1, 1)

        def fr(at):
            return None if at is START else at

        def nxt(at):
            return (at.par + 1) % 2

        def batches(eng, body):
            body(START)
            body(At(0, 0))
            body(At(0, 1))
            with eng.Fori(1, B // 2 - 1) as i:
                body(At(i, 0))
                body(At(i, 1))
            body(At(B // 2 - 1, 0))
            body(At(B // 2 - 1, 1))
            body(None)

        def has_front(at):
            return at is START or not (isinstance(at.i, int) and at.b() == B - 1)

        def following(at):
            return At(at.i, 1) if at.par == 0 else At(at.i + 1, 0)

        LAST = At(B // 2, 0)

        def wait_spread(eng, sems, at, shift=0):
            par = (at.par + shift) % 2
            turn = (at.par + shift - par) // 2
            eng.wait_ge(sems[par], at.i * (16 * H) + 16 * H * (turn + 1))

        def wait_loaded(eng, at, shift):
            par = (at.par + shift) % 2
            turn = (at.par + shift - par) // 2
            eng.wait_ge(loaded[par], at.i * 32 + 32 * (turn + 1))

        block = ctx.enter_context(nc.Block())

        @block.sync
        def _(sp):
            def load(par, b):
                for dst, src in ((G, g), (X, x)):
                    sp.dma_start(dst[:, par, :], src[b]).then_inc(loaded[par], 16)

            def load_turned(b):
                for dst, src in ((XT, xT), (GT, gT)):
                    sp.dma_start(dst[:], src[b].rearrange("(p t) c -> p (t c)", t=T // C)).then_inc(turned_in, 16)
                sp.dma_start(mrow[:], mask[b].rearrange("o (p c k) -> (o c) p k", c=2, k=CH)).then_inc(turned_in, 16)

            def load_mask(b):
                sp.dma_start(maskb[:], mask[b].to_broadcast([C, T])).then_inc(maskb_in, 16)

            sp.dma_start(WL0[:], w_l0.rearrange("p (a c) -> p a c", c=C)).then_inc(consts_in, 16)
            load_turned(0)
            load(0, 0)
            for dst, src in ((WV, w_v.rearrange("p (a c) -> p a c", c=C)), (WQKV, w_qkv.rearrange("p (a c) -> p a c", c=C)),
                             (bcol[:, 0:3], b_col), (ident, consts[:, 0:C]),
                             (onesbd, consts[:, C:C + 2 * D].rearrange("p (c d) -> p c d", c=2)),
                             (Asb[:, 0, 0:CH], consts[:, 160:160 + CH]), (offb, consts[:, 224:224 + C]),
                             (nb, mask_ck), (Msb[0:2, :], indicator)):
                sp.dma_start(dst if dst.__class__ is bass.AP else dst[:], src).then_inc(consts_in, 16)
            sp.dma_start(bv[:], b_v.to_broadcast([C, C])).then_inc(consts_in, 16)
            sp.wait_ge(setup_pool, 1)
            for c in range(2):
                for hh in range(2):
                    for gg in range(4):
                        sp.dma_start(WOZ[32 * gg + D * c:32 * gg + D * c + D, 2 * c + hh, :],
                                     wo[D * (4 * hh + gg):D * (4 * hh + gg) + D, :]).then_inc(consts_in, 16)
            load_mask(0)
            load(1, 1)

            def body(at):
                if at is None:
                    at = LAST
                par, n = at.par, nxt(at)
                if at is START:
                    sp.wait_ge(zeroed_pool, 2)
                elif at.first(-1):
                    sp.wait_ge(zeroed_dve, 2)
                if at is START:
                    wait_use(sp, misc_ready, None, "M", 1)
                    sp.wait_ge(mbias_ready, 1)
                    load_turned(1)
                elif not (isinstance(at.i, int) and at.b(2) >= B):
                    evicted(sp, at, "S")
                    load_turned(at.b(2))
                    load(par, at.b(2))
                if at is not LAST and has_front(at):
                    past(sp, cast_k, at, 2, 1, 2)
                    for h in range(H):
                        sp.dma_start(Kz[n][D * h:D * h + D, h, :], kb[D * h:D * h + D, :]).then_inc(k_spread[n], 16)
                if at is not START and not at.first(-1):
                    past(sp, normed, at, 1, -1, 1)
                    sp.dma_start(out[at.b(-1)], R[:]).then_inc(stored, 16)
                    if at is not LAST:
                        load_mask(at.b())
                if at is not LAST and has_front(at):
                    evicted(sp, fr(at), "q1")
                    for h in range(H):
                        sp.dma_start(Qz[n][D * h:D * h + D, h, :], qs[D * h:D * h + D, :]).then_inc(q_spread[n], 16)

            batches(sp, body)
            sp.wait_ge(stored, 16 * B)

        @block.gpsimd
        def _(pool):
            pool.memset(WOZ[:], 0.0).then_inc(setup_pool, 1)
            pool.memset(Vz[:], 0.0).then_inc(setup_pool, 1)
            pool.memset(halfneg[:], -0.5).then_inc(setup_pool, 1)
            pool.memset(epsc[:], EPS).then_inc(setup_pool, 1)
            pool.memset(Kz0[:], 0.0).then_inc(zeroed_pool, 1)
            pool.memset(Qz0[:], 0.0).then_inc(zeroed_pool, 1)
            pool.wait_ge(setup_pool, 4)
            pool.wait_ge(setup, 4)

            def spread_max(at, p):
                n = NP * at.par + p
                past(pool, mx_taken, at, NP, 0, p + 1)
                past(pool, sc_ready, at, NP, 0, p - 1)
                nc.gpsimd.tensor_tensor(mex[:, n % 2], nmx[:, n % 2, :, None].to_broadcast([C, H, CH]),
                                        i2b[:, None, :].to_broadcast([C, H, CH]), ALU.mult).then_inc(m_ready, 1)

            def tail(at):
                evicted(pool, at, "wo0")
                evicted(pool, at, "wo1")
                nc.gpsimd.tensor_tensor(R[:], R[:], Y[:, nxt(at), :], ALU.add).then_inc(added, 1)

            def root(at):
                past(pool, aggr_done, at, 1, 0, 0)
                nc.gpsimd.tensor_tensor(ve[:], mv[:, 1:2], epsc[:], ALU.add).then_inc(ve_done, 1)
                past(pool, ve_done, at, 1, 0, 0)
                nc.gpsimd.tensor_tensor(rstd[:], ve[:], halfneg[:], ALU.pow).then_inc(rstd_done, 1)

            def body(at):
                if at is START:
                    spread_max(At(0, 0), 0)
                    return
                if at is None:
                    tail(LAST)
                    root(LAST)
                    return
                more = has_front(at)
                for p in range(NP):
                    if p + 1 < NP:
                        spread_max(at, p + 1)
                    elif more:
                        spread_max(following(at), 0)
                    if p == 1 and not at.first(-1):
                        tail(at)
                    if p == 3 and not at.first(-1):
                        root(at)

            batches(pool, body)

        @block.scalar
        def _(act):
            act.wait_ge(consts_in, 16 * NCONST)
            nc.scalar.mul(bcol[:, 3:4], bcol[:, 0:1], SCALE).then_inc(setup_act, 1)
            act.wait_ge(setup, 4)
            act.wait_ge(setup_act, 1)

            def front(at, name):
                n, a = nxt(at), fr(at)
                if name == "M":
                    src = take(act, a, name)
                    nc.scalar.copy(Msb[:], src[:, 0:C]).then_inc(out_sem(a, name), 1)
                if name == "A":
                    src = take(act, a, name)
                    nc.scalar.copy(Asb[:], src[:, 0:2 * C].rearrange("p (a c) -> p a c", a=2)).then_inc(out_sem(a, name), 1)
                if name == "S":
                    past(act, l0_max, at, 1, 1, 1)
                    for d in range(2):
                        nc.scalar.activation(E0[:, d, :], Ssb[:, d, :], ACT.Exp, bias=nmx0[:, d:d + 1],
                                             accum_out=sum0[:, d:d + 1]).then_inc(l0_exp, 1)
                if name == "QA":
                    src = take(act, a, name)
                    past(act, l0_turned, at, 2, 1, 2)
                    for d in range(2):
                        ins = nc.scalar.mul(QAsb[:, d, :], src[:, d * C:d * C + C], rs0[:, d:d + 1])
                    ins.then_inc(out_sem(a, name), 1)
                if name in ("y0", "y1"):
                    j = int(name[1])
                    src = take(act, a, name)
                    if j == 0:
                        past(act, added, at, 1, 0, 0)
                    nc.scalar.copy(Y[:, n, HALF * j:HALF * j + HALF], src[:]).then_inc(out_sem(a, name), 1)
                if name in ("q0", "q1"):
                    j = int(name[1])
                    src = take(act, a, name)
                    if j == 0:
                        past(act, mx_ready, at, NP, 0, 0)
                        past(act, sc_ready, at, NP, 0, 0)
                        if at is not START:
                            wait_spread(act, q_spread, at)
                    cols = slice(HALF * j, HALF * j + HALF)
                    nc.scalar.activation(qb[:, n, cols], src[:], ACT.Identity, bias=bcol[:, 3:4],
                                         scale=SCALE).then_inc(cast_q, 1)
                    nc.scalar.activation(qs[:, cols], src[:], ACT.Identity, bias=bcol[:, 3:4],
                                         scale=SCALE).then_inc(out_sem(a, name), 1)
                if name in ("k0", "k1"):
                    j = int(name[1])
                    src = take(act, a, name)
                    if j == 0:
                        past(act, sc_ready, at, NP, 0, 0)
                        past(act, mx_ready, at, NP, 0, 0)
                        if at is not START:
                            wait_spread(act, k_spread, at)
                    cols = slice(HALF * j, HALF * j + HALF)
                    nc.scalar.activation(kb[:, cols], src[:], ACT.Identity, bias=bcol[:, 1:2]).then_inc(cast_k, 1)
                    nc.scalar.activation(ks[:, n, cols], src[:], ACT.Identity,
                                         bias=bcol[:, 1:2]).then_inc(out_sem(a, name), 1)

            def body(at):
                if at is None:
                    return
                if at is START:
                    for name in FRONT:
                        front(at, name)
                    return
                for p in range(NP):
                    past(act, sc_ready, at, NP, 0, p + 1)
                    past(act, pv_done, at, NP, 0, p - 1)
                    exp_pair(at, p)
                    if has_front(at):
                        for name in PLACE[p]:
                            front(at, name)

            def exp_pair(at, p):
                n = NP * at.par + p
                col = nb[:, bass.ds(at.i * (2 * NP) + n, 1)] if not isinstance(at.i, int) else nb[:, 2 * NP * at.i + n:2 * NP * at.i + n + 1]
                nc.scalar.activation(PT[:, n % PTS, :], SC[n % 2][:], ACT.Exp, bias=col).then_inc(exp_done, 1)

            batches(act, body)

        @block.vector
        def _(dve):
            dve.wait_ge(consts_in, 16 * NCONST)
            dve.tensor_scalar(nb[:], nb[:], 0.0, NEG, ALU.is_le, ALU.mult).then_inc(setup, 1)
            dve.tensor_copy(i2b[:], Asb[:, 0, 0:CH]).then_inc(setup, 1)
            dve.tensor_copy(bones[:], onesbd[:, :, 0, None].to_broadcast([C, 2, CH])).then_inc(setup, 1)
            dve.tensor_copy(indb[:], Msb[0:2, :]).then_inc(setup, 1)
            dve.wait_ge(setup, 4)
            dve.wait_ge(setup_pool, 4)

            def tail(at):
                o = (at.par + 1) % 2
                past(dve, stored, at, 16, -1, 0)
                for c in range(2):
                    src = take(dve, at, f"wo{c}")
                    if c == 0:
                        past(dve, maskb_in, at, 16, 0, 0)
                    m = maskb[:].rearrange("p (n c k) -> p n c k", c=2, k=CH)[:, :, c, :]
                    r = R[:].rearrange("p (n c k) -> p n c k", c=2, k=CH)[:, :, c, :]
                    s = src[:].rearrange("p (n k) -> p n k", k=CH)
                    nc.vector.scalar_tensor_tensor(out=r, in0=s, scalar=bcol[:, 2:3], in1=m, op0=ALU.add,
                                                   op1=ALU.mult).then_inc(out_sem(at, f"wo{c}"), 1)

            def norm(at):
                past(dve, added, at, 1, 0, 0)
                for j in range(2):
                    nc.vector.bn_stats(stats[:, j, :], R[:, HALF * j:HALF * j + HALF]).then_inc(stats_done, 1)
                past(dve, stats_done, at, 2, 0, 0)
                nc.vector.memset(carrier[:], 0.0)
                nc.vector.bn_aggr(mv[:], stats[:].rearrange("p a s -> p (a s)")).then_inc(aggr_done, 1)

            def scale_out(at):
                past(dve, rstd_done, at, 1, 0, 0)
                nc.vector.tensor_scalar(R[:], R[:], mv[:, 0:1], rstd[:, 0:1], ALU.subtract,
                                        ALU.mult).then_inc(normed, 1)

            def mask_rows(at):
                past(dve, turned_in, at, 48, 1, 48)
                past(dve, mx_ready, at, NP, 0, 0)
                nc.vector.tensor_scalar(mbias[:, nxt(at)], mrow[:], 0.0, NEG, ALU.is_le,
                                        ALU.mult).then_inc(mbias_ready, 1)

            def front(at, name):
                n, a = nxt(at), fr(at)
                if name == "S":
                    src = take(dve, a, name)
                    nc.vector.scalar_tensor_tensor(
                        out=Ssb[:], in0=src[:, 0:2 * C].rearrange("p (a c) -> p a c", a=2), scalar=SCALE,
                        in1=offb[:, None, :].to_broadcast([C, 2, C]), op0=ALU.mult, op1=ALU.add).then_inc(out_sem(a, name), 1)
                    evicted(dve, a, name)
                    nc.vector.tensor_reduce(nmx0[:], Ssb[:], AX_X, ALU.max, negate=True).then_inc(l0_max, 1)
                if name == "QA":
                    past(dve, l0_exp, at, 2, 1, 2)
                    nc.vector.reciprocal(rs0[:], sum0[:]).then_inc(l0_turned, 1)
                    nc.vector.transpose(ET[:].rearrange("p a c -> p (a c)"), E0[:].rearrange("p a c -> p (a c)")).then_inc(l0_turned, 1)
                if name == "PM":
                    src = take(dve, a, name)
                    nc.vector.tensor_tensor(WY[:], src[:, 0:2 * C].rearrange("p (a c) -> p a c", a=2),
                                            ident[:, None, :].to_broadcast([C, 2, C]), ALU.add).then_inc(out_sem(a, name), 1)
                if name in ("V0", "V1"):
                    j = int(name[1])
                    src = take(dve, a, name)
                    past(dve, pv_done, at, NP, 0, 0)
                    for c in range(2):
                        rows = slice(CH * c, CH * c + CH)
                        o = Vz[rows, n, 4 * j:4 * j + 4, :, c, :]
                        s = src[rows, :].rearrange("p (n h d) -> p n h d", n=4, d=D)
                        bias = bv[rows, :].rearrange("p (h d) -> p h d", d=D)[:, None].to_broadcast([CH, 4, H, D])
                        ins = nc.vector.tensor_tensor(o, s, bias, ALU.add)
                    ins.then_inc(out_sem(a, name), 1)

            def maxima(at, p):
                n = NP * at.par + p
                past(dve, mx_ready, at, NP, 0, p + 1)
                past(dve, m_ready, at, NP, 0, p - 1)
                nc.vector.tensor_reduce(nmx[:, n % 2, :], MX[n % 2][:].rearrange("p (h k) -> p h k", h=H), AX_X,
                                        ALU.max, negate=True).then_inc(mx_taken, 1)

            def normalise(at, j):
                past(dve, pv_done, at, NP, 0, 4 * j + 4)
                nc.vector.reciprocal(rden[:], DN[:]).then_inc(rden_done, 1)
                past(dve, rden_done, at, 2, 0, j + 1)
                nc.vector.tensor_tensor(On[:, at.par, 4 * j:4 * j + 4].rearrange("p n a q -> p (n a q)"), PVb[:],
                                        rden[:], ALU.mult).then_inc(norm_done, 1)

            def body(at):
                if at is START:
                    mask_rows(at)
                    for name in FRONT:
                        front(at, name)
                    nc.vector.memset(Kz1[:], 0.0).then_inc(zeroed_dve, 1)
                    nc.vector.memset(Qz1[:], 0.0).then_inc(zeroed_dve, 1)
                    maxima(At(0, 0), 0)
                    return
                if at is None:
                    tail(LAST)
                    norm(LAST)
                    scale_out(LAST)
                    return
                more = has_front(at)
                for p in range(NP):
                    if p + 1 < NP:
                        maxima(at, p + 1)
                    elif more:
                        maxima(following(at), 0)
                    if p == 4:
                        normalise(at, 0)
                    if p == 0:
                        if not at.first(-1):
                            tail(at)
                        if more:
                            mask_rows(at)
                    if p == 2 and not at.first(-1):
                        norm(at)
                    if p == 4 and not at.first(-1):
                        scale_out(at)
                    if more:
                        for name in PLACE[p]:
                            front(at, name)
                normalise(at, 1)

            batches(dve, body)

        @block.tensor
        def _(pe):
            pe.wait_ge(consts_in, 16 * NCONST)
            pe.wait_ge(setup, 4)
            pe.wait_ge(setup_pool, 4)

            def front(at, name):
                n, a = nxt(at), fr(at)
                if name == "M":
                    past(pe, turned_in, at, 48, 1, 48)
                if name == "k0":
                    wait_loaded(pe, at, 1)
                dst = put(pe, a, name)
                if name == "M":
                    for t in range(T // C):
                        ins = pe.matmul(dst[:, 0:C], XT[:, C * t:C * t + C], GT[:, C * t:C * t + C],
                                        start=(t == 0), stop=(t == T // C - 1))
                if name == "A":
                    evicted(pe, a, "M")
                    ins = pe.matmul(dst[:, 0:2 * C], Msb[:], WL0[:, 0:2, :], start=True, stop=True)
                if name == "S":
                    evicted(pe, a, "A")
                    pe.matmul(dst[:, 0:C], Asb[:, 0, :], WL0[:, 2, :], start=True, stop=True)
                    ins = pe.matmul(dst[:, C:2 * C], WL0[:, 3, :], Asb[:, 1, :], start=True, stop=True)
                if name == "QA":
                    past(pe, l0_turned, at, 2, 1, 2)
                    pe.matmul(dst[:, 0:C], ET[:, 0, :], WL0[:, 4, :], start=True, stop=True)
                    ins = pe.matmul(dst[:, C:2 * C], ET[:, 1, :], WL0[:, 5, :], start=True, stop=True)
                if name == "PM":
                    evicted(pe, a, "QA")
                    pe.matmul(dst[:, 0:C], WV[:, 0, :], QAsb[:, 0, :], start=True, stop=True)
                    ins = pe.matmul(dst[:, C:2 * C], WV[:, 1, :], QAsb[:, 1, :], start=True, stop=True)
                if name in ("y0", "y1"):
                    evicted(pe, a, "PM")
                    cols = slice(HALF * int(name[1]), HALF * int(name[1]) + HALF)
                    pe.matmul(dst[:], WY[:, 0, :], G[:, n, cols], start=True, stop=False)
                    ins = pe.matmul(dst[:], WY[:, 1, :], X[:, n, cols], start=False, stop=True)
                if name in ("q0", "q1"):
                    cols = slice(HALF * int(name[1]), HALF * int(name[1]) + HALF)
                    ins = pe.matmul(dst[:], WQKV[:, 0, :], G[:, n, cols], start=True, stop=True)
                if name in ("k0", "k1"):
                    cols = slice(HALF * int(name[1]), HALF * int(name[1]) + HALF)
                    ins = pe.matmul(dst[:], WQKV[:, 1, :], G[:, n, cols], start=True, stop=True)
                if name in ("V0", "V1"):
                    for t in range(4):
                        c0 = HALF * int(name[1]) + C * t
                        ins = pe.matmul(dst[:, C * t:C * t + C], G[:, n, c0:c0 + C], WQKV[:, 2, :], start=True, stop=True)
                ins.then_inc(ready_sem(a, name), 1)

            def max_scores(at, p):
                n, par = NP * at.par + p, at.par
                if p == 0:
                    wait_spread(pe, k_spread, at)
                    past(pe, cast_q, at, 2, 0, 2)
                    past(pe, mbias_ready, at, 1, 0, 1)
                past(pe, mx_taken, at, NP, 0, p - 1)
                dst = MX[n % 2]
                for c in range(2):
                    cols = slice(PR * p + CH * c, PR * p + CH * c + CH)
                    pe.matmul(dst[CH * c:CH * c + CH, :], qb[:, par, cols], Kz[par][:, :, cols], start=True,
                              stop=False, skip_group_check=True)
                pe.matmul(dst[:], indb[:], mbias[:, par, p, None, :].to_broadcast([2, H, CH]), start=False, stop=True,
                          skip_group_check=True).then_inc(mx_ready, 1)

            def scores(at, p):
                n, par = NP * at.par + p, at.par
                if p == 0:
                    wait_spread(pe, q_spread, at)
                past(pe, exp_done, at, NP, 0, p - 1)
                dst = SC[n % 2]
                for c in range(2):
                    cols = slice(PR * p + CH * c, PR * p + CH * c + CH)
                    pe.matmul(dst[CH * c:CH * c + CH, :], ks[:, par, cols], Qz[par][:, :, cols], start=True,
                              stop=False, skip_group_check=True)
                past(pe, m_ready, at, NP, 0, p + 1)
                pe.matmul(dst[:], bones[:].rearrange("p c k -> p (c k)"), mex[:, n % 2].rearrange("p h q -> p (h q)"),
                          start=False, stop=True, skip_group_check=True).then_inc(sc_ready, 1)

            def outputs(at, p):
                n, par = NP * at.par + p, at.par
                past(pe, exp_done, at, NP, 0, p + 1)
                if p % 4 == 0:
                    past(pe, norm_done, at, 2, 0, p // 4)
                for h in range(H):
                    gg, hh = h % 4, h // 4
                    c0 = PR * (p % 4) + CH * hh
                    pe.matmul(PVb[32 * gg:32 * gg + 32, c0:c0 + CH], Vz[:, par, p, h].rearrange("p c d -> p (c d)"),
                              PT[:, n % PTS, CH * h:CH * h + CH], start=True, stop=True, tile_position=(0, 32 * gg))
                for gg in range(4):
                    rhs = PT[:, n % PTS, :].rearrange("p (a g q) -> p a g q", a=2, g=4)[:, :, gg, :]
                    ins = pe.matmul(DN[32 * gg:32 * gg + 32, PR * (p % 4):PR * (p % 4) + PR],
                                    onesbd[:].rearrange("p c d -> p (c d)"), rhs, start=True, stop=True,
                                    tile_position=(0, 32 * gg))
                ins.then_inc(pv_done, 1)

            def tail(at):
                o = (at.par + 1) % 2
                for c in range(2):
                    dst = put(pe, at, f"wo{c}")
                    if c == 0:
                        past(pe, norm_done, at, 2, 0, 0)
                    for hh in range(2):
                        ins = pe.matmul(dst[:], WOZ[:, 2 * c + hh, :], On[:, o, :, hh, :], start=(hh == 0), stop=(hh == 1))
                    ins.then_inc(ready_sem(at, f"wo{c}"), 1)

            def body(at):
                if at is START:
                    for name in FRONT:
                        front(at, name)
                    max_scores(At(0, 0), 0)
                    return
                if at is None:
                    tail(LAST)
                    return
                more = has_front(at)
                for p in range(NP):
                    scores(at, p)
                    if p + 1 < NP:
                        max_scores(at, p + 1)
                    elif more:
                        max_scores(following(at), 0)
                    if p:
                        outputs(at, p - 1)
                    if p == 0 and not at.first(-1):
                        tail(at)
                    if more:
                        for name in PLACE[p]:
                            front(at, name)
                outputs(at, NP - 1)

            batches(pe, body)


def kernel(**inputs):
    import numpy as np
    import concourse.bacc as bacc
    from concourse.bass_utils import run_bass_kernel_spmd

    a = {n: np.asarray(v) for n, v in inputs.items()}
    x, g, mask = a["x"], a["ctx_4096"], a["mask_Bx1x4096_ff1"]
    w = {n[len("L0_xattn_"):]: v for n, v in a.items() if n.startswith("L0_xattn_")}
    b_in = a["L1_xattn_b_in"]

    row = np.arange(C)
    consts = np.zeros((C, 224 + C), np.float32)
    consts[:, 0:C] = np.eye(C)
    consts[:, C:C + 2 * D] = row[:, None] // CH == np.arange(2 * D)[None, :] // D
    consts[:, 160:160 + CH] = row[:, None] % CH == np.arange(CH)[None, :]
    consts[:, 224:224 + C] = np.where(row[:, None] // D == row[None, :] // D, 0.0, OFF)
    indicator = (np.arange(2)[:, None] == row[None, :] // CH).astype(np.float32)

    arrays = {
        "x_in": x, "g_in": g, "xT_in": x.transpose(0, 2, 1), "gT_in": g.transpose(0, 2, 1), "mask_in": mask,
        "mask_ck_in": mask.reshape(B, NP, PR).transpose(2, 0, 1).reshape(PR, B * NP),
        "w_l0_in": np.concatenate([w["wq_rgb"].T, w["wk_rgb"].T, w["wk_point"].T, w["wq_point"].T,
                                   w["proj_p2r"].T, w["proj_r2p"].T], axis=1),
        "w_v_in": np.concatenate([w["wv_point"], w["wv_rgb"]], axis=1),
        "w_qkv_in": a["L1_xattn_W_in"].T, "wo_in": a["L1_xattn_W_out"].T,
        "b_col_in": np.stack([b_in[0:C], b_in[C:2 * C], a["L1_xattn_b_out"]], axis=1),
        "b_v_in": b_in[2 * C:3 * C].reshape(1, C), "consts_in": consts, "indicator_in": indicator,
    }
    arrays = {n: np.ascontiguousarray(v) for n, v in arrays.items()}
    nc = bacc.Bacc("TRN2", target_bir_lowering=False, num_devices=1)
    args = [nc.dram_tensor(n, v.shape, mybir.dt.from_np(v.dtype), kind="ExternalInput").ap() for n, v in arrays.items()]
    args.append(nc.dram_tensor("y_out", (B, C, T), F32, kind="ExternalOutput").ap())
    program(nc, *args)
    r = run_bass_kernel_spmd(nc, [arrays], core_ids=[0])
    return r.results[0]["y_out"]
```

```python
from contextlib import ExitStack

import concourse.bass as bass
from concourse import mybir

B, C, T, H = 16, 128, 1024, 8
D = C // H
CH = 64
PR = 2 * CH
NP = T // PR
HALF = T // 2
SCALE = float(D) ** -0.5
NEG = -1.0e9
PTS = 2
LEAD = 2
OFF = -1.0e30
EPS = 1e-5

F32 = mybir.dt.float32
BF16 = mybir.dt.bfloat16
ALU = mybir.AluOpType
ACT = mybir.ActivationFunctionType
AX_X = mybir.AxisListType.X

ORDER = ["k0", "k1", "q0", "M", "q1", "A", "V0", "S", "wo0", "wo1", "V1", "QA", "PM", "y0", "y1"]
TAIL = ORDER[8:10]
FRONT = ORDER[:8] + ORDER[10:]
PLACE = {0: ["k0", "k1"], 1: ["q0", "M", "q1"], 2: ["A", "V0"], 3: ["S"], 4: ["V1"], 5: ["QA"],
         6: ["PM"], 7: ["y0", "y1"]}
TURN_AT = 3
TAIL_AT = 4
USES = len(ORDER)
FIRST = 3 * C + 2 * D + CH + 4


def program(nc, x, g, xT, gT, mask, mask_ck, w_first, w_second, wo, b_v, indicator, out):
    with ExitStack() as ctx:
        def sb(name, shape, dt=F32):
            return ctx.enter_context(nc.sbuf_tensor(name, shape, dt))

        def ps(name):
            return ctx.enter_context(nc.psum_tensor(name, [C, HALF], F32))

        def sem(name):
            return ctx.enter_context(nc.semaphore(name))

        X = sb("X", [C, 2, T])
        G = sb("G", [C, 2, T])
        XT = sb("XT", [C, T])
        GT = sb("GT", [C, T])
        mrow = sb("mrow", [2, NP, CH])
        first = sb("first", [C, FIRST])
        WQKV = first[:, 0:3 * C].rearrange("p (a c) -> p a c", c=C)
        onesbd = first[:, 3 * C:3 * C + 2 * D].rearrange("p (c d) -> p c d", c=2)
        bcol = first[:, FIRST - 4:FIRST]
        second = sb("second", [C, 10, C])
        WL0 = second[:, 0:6, :]
        WV = second[:, 6:8, :]
        ident, offb = second[:, 8, :], second[:, 9, :]
        WOZ = sb("WOZ", [C, 4, C])
        bv = sb("bv", [C, C])
        i2b = sb("i2b", [C, CH], BF16)
        indb = sb("indb", [2, C], BF16)
        nb = sb("nb", [C, B * NP])
        halfneg = sb("halfneg", [C, 1])
        epsc = sb("epsc", [C, 1])
        carrier = sb("carrier", [C, 1])
        Msb = sb("Msb", [C, C])
        Asb = sb("Asb", [C, 2, C])
        Ssb = sb("Ssb", [C, 2, C])
        nmx0 = sb("nmx0", [C, 2])
        E0 = sb("E0", [C, 2, C])
        sum0 = sb("sum0", [C, 2])
        rs0 = sb("rs0", [C, 2])
        ET = sb("ET", [C, 2, C])
        QAsb = sb("QAsb", [C, 2, C])
        WY = sb("WY", [C, 2, C])
        Y = sb("Y", [C, 2, T])
        qs = sb("qs", [C, T])
        qb = sb("qb", [C, 2, T], BF16)
        ks = sb("ks", [C, 2, T])
        kb = sb("kb", [C, T], BF16)
        Qz0, Qz1 = sb("Qz0", [C, H, T]), sb("Qz1", [C, H, T])
        Kz0, Kz1 = sb("Kz0", [C, H, T], BF16), sb("Kz1", [C, H, T], BF16)
        Qz, Kz = [Qz0, Qz1], [Kz0, Kz1]
        Vz = sb("Vz", [C, 2, NP, H, 2, D])
        mbias = sb("mbias", [2, 2, NP, CH], BF16)
        nmx = sb("nmx", [C, 2, H], BF16)
        mex = sb("mex", [C, 2, H, CH], BF16)
        bones = sb("bones", [C, 2, CH], BF16)
        PT = sb("PT", [C, PTS, HALF])
        den = sb("den", [C, HALF])
        On = sb("On", [C, 2, NP, 2, CH])
        R = sb("R", [C, T])
        maskb = sb("maskb", [C, T])
        stats = sb("stats", [C, 2, 6])
        mv = sb("mv", [C, 2])
        ve = sb("ve", [C, 1])
        rstd = sb("rstd", [C, 1])

        misc = [ps("misc0"), ps("misc1")]
        MX = [ps("mx0"), ps("mx1")]
        SC = [ps("sc0"), ps("sc1")]
        PVb, DN = ps("pv"), ps("dn")

        first_in = sem("first_in")
        consts_in = sem("consts_in")
        wo_in = sem("wo_in")
        setup = sem("setup")
        setup_pool = sem("setup_pool")
        setup_act = sem("setup_act")
        zeroed_pool, zeroed_dve = sem("zeroed_pool"), sem("zeroed_dve")
        maskb_in = sem("maskb_in")
        turned_in = sem("turned_in")
        loaded = [sem("loaded0"), sem("loaded1")]
        misc_ready = [sem("misc_ready0"), sem("misc_ready1")]
        misc_out = [sem("misc_out0"), sem("misc_out1")]
        l0_max, l0_exp, l0_turned = sem("l0_max"), sem("l0_exp"), sem("l0_turned")
        cast_k, cast_q = sem("cast_k"), sem("cast_q")
        q_spread = [sem("q_spread0"), sem("q_spread1")]
        k_spread = [sem("k_spread0"), sem("k_spread1")]
        mbias_ready = sem("mbias_ready")
        mx_ready, mx_taken, m_ready = sem("mx_ready"), sem("mx_taken"), sem("m_ready")
        sc_ready, exp_done = sem("sc_ready"), sem("exp_done")
        pv_done = sem("pv_done")
        den_out, raw_out = sem("den_out"), sem("raw_out")
        rden_done, norm_done = sem("rden_done"), sem("norm_done")
        added = sem("added")
        stats_done, aggr_done, ve_done, rstd_done = sem("stats_done"), sem("aggr_done"), sem("ve_done"), sem("rstd_done")
        normed = sem("normed")
        stored = sem("stored")


        class At:
            def __init__(self, i, par):
                self.i, self.par = i, par

            def b(self, shift=0):
                return self.i * 2 + (self.par + shift)

            def first(self, shift=0):
                return isinstance(self.i, int) and self.b(shift) < 0

        def past(eng, s, at, per, shift, extra):
            if isinstance(at.i, int) and per * at.b(shift) + extra <= 0:
                return
            eng.wait_ge(s, at.i * (2 * per) + (per * (at.par + shift) + extra))

        def use(at, name):
            front, tail, base = len(FRONT), len(TAIL), 0
            if at is None:
                n = FRONT.index(name)
            elif not isinstance(at.i, int):
                n, base = 2 * front - USES + USES * at.par + ORDER.index(name), at.i * USES
            elif at.b() == 0:
                n = front + FRONT.index(name)
            else:
                n = 2 * front + USES * (at.b() - 1)
                if at.b() >= B - 1:
                    n += TAIL.index(name) - (front if at.b() == B else 0)
                else:
                    n += ORDER.index(name)
            return n % 2, n // 2, base

        def wait_use(eng, sems, at, name, back):
            bank, turn, base = use(at, name)
            if isinstance(base, int) and base + turn + back <= 0:
                return
            eng.wait_ge(sems[bank], base + (turn + back))

        def take(eng, at, name):
            wait_use(eng, misc_ready, at, name, 1)
            return misc[use(at, name)[0]]

        def put(eng, at, name):
            wait_use(eng, misc_out, at, name, 0)
            return misc[use(at, name)[0]]

        def evicted(eng, at, name):
            wait_use(eng, misc_out, at, name, 1)

        def out_sem(at, name):
            return misc_out[use(at, name)[0]]

        def ready_sem(at, name):
            return misc_ready[use(at, name)[0]]

        START = At(-1, 1)

        def fr(at):
            return None if at is START else at

        def nxt(at):
            return (at.par + 1) % 2

        def batches(eng, body):
            body(START)
            body(At(0, 0))
            body(At(0, 1))
            with eng.Fori(1, B // 2 - 1) as i:
                body(At(i, 0))
                body(At(i, 1))
            body(At(B // 2 - 1, 0))
            body(At(B // 2 - 1, 1))
            body(None)

        def has_front(at):
            return at is START or not (isinstance(at.i, int) and at.b() == B - 1)

        def following(at):
            return At(at.i, 1) if at.par == 0 else At(at.i + 1, 0)

        def ahead(at, p):
            return (at, p + LEAD) if p + LEAD < NP else (following(at), p + LEAD - NP)

        LAST = At(B // 2, 0)

        def wait_spread(eng, sems, at, shift=0):
            par = (at.par + shift) % 2
            turn = (at.par + shift - par) // 2
            eng.wait_ge(sems[par], at.i * (16 * H) + 16 * H * (turn + 1))

        def wait_loaded(eng, at, shift):
            par = (at.par + shift) % 2
            turn = (at.par + shift - par) // 2
            eng.wait_ge(loaded[par], at.i * 32 + 32 * (turn + 1))

        block = ctx.enter_context(nc.Block())

        @block.sync
        def _(sp):
            def load(par, b):
                for dst, src in ((G, g), (X, x)):
                    sp.dma_start(dst[:, par, :], src[b]).then_inc(loaded[par], 16)

            def load_turned(b):
                for dst, src in ((XT, xT), (GT, gT)):
                    sp.dma_start(dst[:], src[b].rearrange("(p t) c -> p (t c)", t=T // C)).then_inc(turned_in, 16)
                sp.dma_start(mrow[:], mask[b].rearrange("o (p c k) -> (o c) p k", c=2, k=CH)).then_inc(turned_in, 16)

            def load_mask(b):
                sp.dma_start(maskb[:], mask[b].to_broadcast([C, T])).then_inc(maskb_in, 16)

            sp.dma_start(first[:], w_first).then_inc(first_in, 16)
            sp.dma_start(Msb[0:2, :], indicator).then_inc(first_in, 16)
            load(0, 0)
            sp.dma_start(bv[:], b_v.to_broadcast([C, C])).then_inc(first_in, 16)
            load_turned(0)
            sp.dma_start(second[:], w_second.rearrange("p (a c) -> p a c", c=C)).then_inc(consts_in, 16)
            sp.dma_start(nb[:], mask_ck).then_inc(consts_in, 16)
            load(1, 1)

            def load_wo():
                for c in range(2):
                    for hh in range(2):
                        for gg in range(4):
                            sp.dma_start(WOZ[32 * gg + D * c:32 * gg + D * c + D, 2 * c + hh, :],
                                         wo[D * (4 * hh + gg):D * (4 * hh + gg) + D, :]).then_inc(wo_in, 16)
                load_mask(0)

            def body(at):
                if at is None:
                    at = LAST
                par, n = at.par, nxt(at)
                if isinstance(at.i, int) and at.b() == 0:
                    sp.wait_ge(setup_pool, 4)
                    load_wo()
                more = not (at is LAST or isinstance(at.i, int) and at.b(2) >= B)
                if at is not START and more:
                    wait_use(sp, misc_ready, at, "k0", 1)
                    load(par, at.b(2))
                if at is START:
                    sp.wait_ge(zeroed_dve, 1)
                elif at.first(-1):
                    sp.wait_ge(zeroed_pool, 2)
                if at is not LAST and has_front(at):
                    past(sp, cast_k, at, 2, 1, 2)
                    for h in range(H):
                        sp.dma_start(Kz[n][D * h:D * h + D, h, :], kb[D * h:D * h + D, :]).then_inc(k_spread[n], 16)
                    if at is START:
                        sp.wait_ge(zeroed_dve, 3)
                    evicted(sp, fr(at), "q1")
                    for h in range(H):
                        sp.dma_start(Qz[n][D * h:D * h + D, h, :], qs[D * h:D * h + D, :]).then_inc(q_spread[n], 16)
                if more:
                    evicted(sp, fr(at), "S")
                    load_turned(at.b(2))
                if at is not START and not at.first(-1):
                    past(sp, normed, at, 1, -1, 1)
                    sp.dma_start(out[at.b(-1)], R[:]).then_inc(stored, 16)
                    if at is not LAST:
                        load_mask(at.b())
            batches(sp, body)
            sp.wait_ge(stored, 16 * B)

        @block.gpsimd
        def _(pool):
            pool.memset(WOZ[:], 0.0).then_inc(setup_pool, 1)
            pool.memset(Vz[:, 1], 0.0).then_inc(setup_pool, 1)
            pool.memset(halfneg[:], -0.5).then_inc(setup_pool, 1)
            pool.memset(epsc[:], EPS).then_inc(setup_pool, 1)
            pool.memset(Kz1[:].bitcast(F32), 0.0).then_inc(zeroed_pool, 1)
            pool.memset(Qz1[:], 0.0).then_inc(zeroed_pool, 1)
            pool.wait_ge(setup_pool, 4)
            pool.wait_ge(setup, 3)

            def spread_max(at, p):
                n = NP * at.par + p
                past(pool, mx_taken, at, NP, 0, p + 1)
                past(pool, sc_ready, at, NP, 0, p - 1)
                nc.gpsimd.tensor_tensor(mex[:, n % 2], nmx[:, n % 2, :, None].to_broadcast([C, H, CH]),
                                        i2b[:, None, :].to_broadcast([C, H, CH]), ALU.mult).then_inc(m_ready, 1)

            def tail(at):
                evicted(pool, at, "wo0")
                evicted(pool, at, "wo1")
                nc.gpsimd.tensor_tensor(R[:], R[:], Y[:, nxt(at), :], ALU.add).then_inc(added, 1)

            def root(at):
                past(pool, aggr_done, at, 1, 0, 0)
                nc.gpsimd.tensor_tensor(ve[:], mv[:, 1:2], epsc[:], ALU.add).then_inc(ve_done, 1)
                past(pool, ve_done, at, 1, 0, 0)
                nc.gpsimd.tensor_tensor(rstd[:], ve[:], halfneg[:], ALU.pow).then_inc(rstd_done, 1)

            def body(at):
                if at is START:
                    for p in range(LEAD):
                        spread_max(At(0, 0), p)
                    return
                if at is None:
                    tail(LAST)
                    root(LAST)
                    return
                more = has_front(at)
                for p in range(NP):
                    if p + LEAD < NP or more:
                        spread_max(*ahead(at, p))
                    if p == TAIL_AT + 1 and not at.first(-1):
                        tail(at)
                    if p == TAIL_AT + 2 and not at.first(-1):
                        root(at)

            batches(pool, body)

        @block.scalar
        def _(act):
            act.wait_ge(first_in, 48)
            nc.scalar.mul(bcol[:, 3:4], bcol[:, 0:1], SCALE).then_inc(setup_act, 1)
            act.wait_ge(setup, 3)
            act.wait_ge(setup_act, 1)

            def front(at, name):
                n, a = nxt(at), fr(at)
                if name == "M":
                    src = take(act, a, name)
                    nc.scalar.copy(Msb[:], src[:, 0:C]).then_inc(out_sem(a, name), 1)
                if name == "A":
                    src = take(act, a, name)
                    nc.scalar.copy(Asb[:], src[:, 0:2 * C].rearrange("p (a c) -> p a c", a=2)).then_inc(out_sem(a, name), 1)
                if name == "S":
                    past(act, l0_max, at, 1, 1, 1)
                    for d in range(2):
                        nc.scalar.activation(E0[:, d, :], Ssb[:, d, :], ACT.Exp, bias=nmx0[:, d:d + 1],
                                             accum_out=sum0[:, d:d + 1]).then_inc(l0_exp, 1)
                if name == "QA":
                    src = take(act, a, name)
                    past(act, l0_turned, at, 2, 1, 2)
                    for d in range(2):
                        ins = nc.scalar.mul(QAsb[:, d, :], src[:, d * C:d * C + C], rs0[:, d:d + 1])
                    ins.then_inc(out_sem(a, name), 1)
                if name in ("y0", "y1"):
                    j = int(name[1])
                    src = take(act, a, name)
                    if j == 0:
                        past(act, added, at, 1, 0, 0)
                    nc.scalar.copy(Y[:, n, HALF * j:HALF * j + HALF], src[:]).then_inc(out_sem(a, name), 1)
                if name in ("q0", "q1"):
                    j = int(name[1])
                    src = take(act, a, name)
                    if j == 0:
                        past(act, mx_ready, at, NP, 0, 0)
                        past(act, sc_ready, at, NP, 0, 0)
                        if at is not START:
                            wait_spread(act, q_spread, at)
                    cols = slice(HALF * j, HALF * j + HALF)
                    nc.scalar.activation(qb[:, n, cols], src[:], ACT.Identity, bias=bcol[:, 3:4],
                                         scale=SCALE).then_inc(cast_q, 1)
                    nc.scalar.activation(qs[:, cols], src[:], ACT.Identity, bias=bcol[:, 3:4],
                                         scale=SCALE).then_inc(out_sem(a, name), 1)
                if name in ("k0", "k1"):
                    j = int(name[1])
                    src = take(act, a, name)
                    if j == 0:
                        past(act, sc_ready, at, NP, 0, 0)
                        past(act, mx_ready, at, NP, 0, 0)
                        if at is not START:
                            wait_spread(act, k_spread, at)
                    cols = slice(HALF * j, HALF * j + HALF)
                    nc.scalar.activation(kb[:, cols], src[:], ACT.Identity, bias=bcol[:, 1:2]).then_inc(cast_k, 1)
                    nc.scalar.activation(ks[:, n, cols], src[:], ACT.Identity,
                                         bias=bcol[:, 1:2]).then_inc(out_sem(a, name), 1)

            def body(at):
                if at is None:
                    return
                if at is START:
                    for name in FRONT:
                        front(at, name)
                    return
                for p in range(NP):
                    past(act, sc_ready, at, NP, 0, p + 1)
                    past(act, pv_done, at, NP, 0, p - 1)
                    exp_pair(at, p)
                    if p == 4:
                        sums(at, 0)
                    if has_front(at):
                        for name in PLACE[p]:
                            front(at, name)
                sums(at, 1)

            def sums(at, j):
                past(act, pv_done, at, NP, 0, 4 * j + 4)
                past(act, norm_done, at, NP, 0, 4 * j)
                nc.scalar.copy(den[:], DN[:]).then_inc(den_out, 1)
                nc.scalar.copy(On[:, at.par, 4 * j:4 * j + 4].rearrange("p n a q -> p (n a q)"),
                               PVb[:]).then_inc(raw_out, 1)

            def exp_pair(at, p):
                n = NP * at.par + p
                col = nb[:, bass.ds(at.i * (2 * NP) + n, 1)] if not isinstance(at.i, int) else nb[:, 2 * NP * at.i + n:2 * NP * at.i + n + 1]
                nc.scalar.activation(PT[:, n % PTS, :], SC[n % 2][:], ACT.Exp, bias=col).then_inc(exp_done, 1)

            batches(act, body)

        @block.vector
        def _(dve):
            dve.memset(Kz0[:].bitcast(F32), 0.0).then_inc(zeroed_dve, 1)
            dve.memset(Vz[:, 0], 0.0).then_inc(zeroed_dve, 1)
            dve.wait_ge(first_in, 48)
            dve.tensor_copy(i2b[:], first[:, FIRST - 4 - CH:FIRST - 4]).then_inc(setup, 1)
            dve.tensor_copy(bones[:], onesbd[:, :, 0:1].to_broadcast([C, 2, CH])).then_inc(setup, 1)
            dve.tensor_copy(indb[:], Msb[0:2, :]).then_inc(setup, 1)
            dve.memset(Qz0[:], 0.0).then_inc(zeroed_dve, 1)
            dve.wait_ge(consts_in, 32)
            dve.tensor_scalar(nb[:], nb[:], 0.0, NEG, ALU.is_le, ALU.mult).then_inc(setup, 1)
            dve.wait_ge(setup, 4)
            dve.wait_ge(setup_pool, 4)

            def tail(at):
                o = (at.par + 1) % 2
                past(dve, stored, at, 16, -1, 0)
                for c in range(2):
                    src = take(dve, at, f"wo{c}")
                    if c == 0:
                        past(dve, maskb_in, at, 16, 0, 0)
                    m = maskb[:].rearrange("p (n c k) -> p n c k", c=2, k=CH)[:, :, c, :]
                    r = R[:].rearrange("p (n c k) -> p n c k", c=2, k=CH)[:, :, c, :]
                    s = src[:].rearrange("p (n k) -> p n k", k=CH)
                    nc.vector.scalar_tensor_tensor(out=r, in0=s, scalar=bcol[:, 2:3], in1=m, op0=ALU.add,
                                                   op1=ALU.mult).then_inc(out_sem(at, f"wo{c}"), 1)

            def norm(at):
                past(dve, added, at, 1, 0, 0)
                for j in range(2):
                    nc.vector.bn_stats(stats[:, j, :], R[:, HALF * j:HALF * j + HALF]).then_inc(stats_done, 1)
                past(dve, stats_done, at, 2, 0, 0)
                nc.vector.memset(carrier[:], 0.0)
                nc.vector.bn_aggr(mv[:], stats[:].rearrange("p a s -> p (a s)")).then_inc(aggr_done, 1)

            def scale_out(at):
                past(dve, rstd_done, at, 1, 0, 0)
                nc.vector.tensor_scalar(R[:], R[:], mv[:, 0:1], rstd[:, 0:1], ALU.subtract,
                                        ALU.mult).then_inc(normed, 1)

            def mask_rows(at):
                past(dve, turned_in, at, 48, 1, 48)
                past(dve, mx_ready, at, NP, 0, 0)
                nc.vector.tensor_scalar(mbias[:, nxt(at)], mrow[:], 0.0, NEG, ALU.is_le,
                                        ALU.mult).then_inc(mbias_ready, 1)

            def front(at, name):
                n, a = nxt(at), fr(at)
                if name == "S":
                    src = take(dve, a, name)
                    nc.vector.scalar_tensor_tensor(
                        out=Ssb[:], in0=src[:, 0:2 * C].rearrange("p (a c) -> p a c", a=2), scalar=SCALE,
                        in1=offb[:, None, :].to_broadcast([C, 2, C]), op0=ALU.mult, op1=ALU.add).then_inc(out_sem(a, name), 1)
                    evicted(dve, a, name)
                    nc.vector.tensor_reduce(nmx0[:], Ssb[:], AX_X, ALU.max, negate=True).then_inc(l0_max, 1)
                if name == "turn":
                    past(dve, l0_exp, at, 2, 1, 2)
                    nc.vector.reciprocal(rs0[:], sum0[:]).then_inc(l0_turned, 1)
                    nc.vector.transpose(ET[:].rearrange("p a c -> p (a c)"), E0[:].rearrange("p a c -> p (a c)")).then_inc(l0_turned, 1)
                if name == "PM":
                    src = take(dve, a, name)
                    nc.vector.tensor_tensor(WY[:], src[:, 0:2 * C].rearrange("p (a c) -> p a c", a=2),
                                            ident[:, None, :].to_broadcast([C, 2, C]), ALU.add).then_inc(out_sem(a, name), 1)
                if name in ("V0", "V1"):
                    j = int(name[1])
                    src = take(dve, a, name)
                    past(dve, pv_done, at, NP, 0, 0)
                    for c in range(2):
                        rows = slice(CH * c, CH * c + CH)
                        o = Vz[rows, n, 4 * j:4 * j + 4, :, c, :]
                        s = src[rows, :].rearrange("p (n h d) -> p n h d", n=4, d=D)
                        bias = bv[rows, :].rearrange("p (h d) -> p h d", d=D)[:, None].to_broadcast([CH, 4, H, D])
                        ins = nc.vector.tensor_tensor(o, s, bias, ALU.add)
                    ins.then_inc(out_sem(a, name), 1)

            def maxima(at, p):
                n = NP * at.par + p
                past(dve, mx_ready, at, NP, 0, p + 1)
                past(dve, m_ready, at, NP, 0, p - 1)
                nc.vector.tensor_reduce(nmx[:, n % 2, :], MX[n % 2][:].rearrange("p (h k) -> p h k", h=H), AX_X,
                                        ALU.max, negate=True).then_inc(mx_taken, 1)

            def normalise(at, j):
                half, part = j // 4, j % 4
                cols = slice(PR * part, PR * part + PR)
                if part == 0:
                    past(dve, den_out, at, 2, 0, half + 1)
                nc.vector.reciprocal(den[:, cols], den[:, cols]).then_inc(rden_done, 1)
                if part == 0:
                    past(dve, raw_out, at, 2, 0, half + 1)
                past(dve, rden_done, at, NP, 0, j + 1)
                o = On[:, at.par % 2, j].rearrange("p a q -> p (a q)")
                nc.vector.tensor_tensor(o, o, den[:, cols], ALU.mult).then_inc(norm_done, 1)

            def before(at):
                return At(at.i, 0) if at.par == 1 else At(at.i + (-1), 1)

            def body(at):
                if at is START:
                    mask_rows(at)
                    for name in FRONT:
                        if name == "QA":
                            front(at, "turn")
                        front(at, name)
                    for p in range(LEAD):
                        maxima(At(0, 0), p)
                    return
                if at is None:
                    for j in range(4, NP):
                        normalise(before(LAST), j)
                    tail(LAST)
                    norm(LAST)
                    scale_out(LAST)
                    return
                more = has_front(at)
                for p in range(NP):
                    if p + LEAD < NP or more:
                        maxima(*ahead(at, p))
                    if p == 0 and more:
                        mask_rows(at)
                    if p >= 4:
                        normalise(at, p - 4)
                    elif not at.first(-1):
                        normalise(before(at), p + 4)
                    if not at.first(-1):
                        if p == TAIL_AT:
                            tail(at)
                    if more:
                        for name in PLACE[p] + (["turn"] if p == TURN_AT else []):
                            front(at, name)
                    if not at.first(-1):
                        if p == TAIL_AT + 2:
                            norm(at)
                        if p == TAIL_AT + 3:
                            scale_out(at)

            batches(dve, body)

        @block.tensor
        def _(pe):
            pe.wait_ge(first_in, 48)
            pe.wait_ge(setup, 3)

            def front(at, name):
                n, a = nxt(at), fr(at)
                if name == "M":
                    past(pe, turned_in, at, 48, 1, 48)
                if name == "k0":
                    wait_loaded(pe, at, 1)
                dst = put(pe, a, name)
                if name == "M":
                    if at is START:
                        pe.wait_ge(consts_in, 32)
                    for t in range(T // C):
                        ins = pe.matmul(dst[:, 0:C], XT[:, C * t:C * t + C], GT[:, C * t:C * t + C],
                                        start=(t == 0), stop=(t == T // C - 1))
                if name == "A":
                    evicted(pe, a, "M")
                    ins = pe.matmul(dst[:, 0:2 * C], Msb[:], WL0[:, 0:2, :], start=True, stop=True)
                if name == "S":
                    evicted(pe, a, "A")
                    pe.matmul(dst[:, 0:C], Asb[:, 0, :], WL0[:, 2, :], start=True, stop=True)
                    ins = pe.matmul(dst[:, C:2 * C], WL0[:, 3, :], Asb[:, 1, :], start=True, stop=True)
                if name == "QA":
                    past(pe, l0_turned, at, 2, 1, 2)
                    pe.matmul(dst[:, 0:C], ET[:, 0, :], WL0[:, 4, :], start=True, stop=True)
                    ins = pe.matmul(dst[:, C:2 * C], ET[:, 1, :], WL0[:, 5, :], start=True, stop=True)
                if name == "PM":
                    evicted(pe, a, "QA")
                    pe.matmul(dst[:, 0:C], WV[:, 0, :], QAsb[:, 0, :], start=True, stop=True)
                    ins = pe.matmul(dst[:, C:2 * C], WV[:, 1, :], QAsb[:, 1, :], start=True, stop=True)
                if name in ("y0", "y1"):
                    evicted(pe, a, "PM")
                    cols = slice(HALF * int(name[1]), HALF * int(name[1]) + HALF)
                    pe.matmul(dst[:], WY[:, 0, :], G[:, n, cols], start=True, stop=False)
                    ins = pe.matmul(dst[:], WY[:, 1, :], X[:, n, cols], start=False, stop=True)
                if name in ("q0", "q1"):
                    cols = slice(HALF * int(name[1]), HALF * int(name[1]) + HALF)
                    ins = pe.matmul(dst[:], WQKV[:, 0, :], G[:, n, cols], start=True, stop=True)
                if name in ("k0", "k1"):
                    cols = slice(HALF * int(name[1]), HALF * int(name[1]) + HALF)
                    ins = pe.matmul(dst[:], WQKV[:, 1, :], G[:, n, cols], start=True, stop=True)
                if name in ("V0", "V1"):
                    for t in range(4):
                        c0 = HALF * int(name[1]) + C * t
                        ins = pe.matmul(dst[:, C * t:C * t + C], G[:, n, c0:c0 + C], WQKV[:, 2, :], start=True, stop=True)
                ins.then_inc(ready_sem(a, name), 1)

            def max_scores(at, p):
                n, par = NP * at.par + p, at.par
                if p == 0:
                    wait_spread(pe, k_spread, at)
                    past(pe, cast_q, at, 2, 0, 2)
                    past(pe, mbias_ready, at, 1, 0, 1)
                past(pe, mx_taken, at, NP, 0, p - 1)
                dst = MX[n % 2]
                for c in range(2):
                    cols = slice(PR * p + CH * c, PR * p + CH * c + CH)
                    pe.matmul(dst[CH * c:CH * c + CH, :], qb[:, par, cols], Kz[par][:, :, cols], start=True,
                              stop=False, skip_group_check=True)
                pe.matmul(dst[:], indb[:], mbias[:, par, p, None, :].to_broadcast([2, H, CH]), start=False, stop=True,
                          skip_group_check=True).then_inc(mx_ready, 1)

            def scores(at, p):
                n, par = NP * at.par + p, at.par
                if p == 0:
                    wait_spread(pe, q_spread, at)
                past(pe, exp_done, at, NP, 0, p - 1)
                dst = SC[n % 2]
                for c in range(2):
                    cols = slice(PR * p + CH * c, PR * p + CH * c + CH)
                    pe.matmul(dst[CH * c:CH * c + CH, :], ks[:, par, cols], Qz[par][:, :, cols], start=True,
                              stop=False, skip_group_check=True)
                past(pe, m_ready, at, NP, 0, p + 1)
                pe.matmul(dst[:], bones[:].rearrange("p c k -> p (c k)"), mex[:, n % 2].rearrange("p h q -> p (h q)"),
                          start=False, stop=True, skip_group_check=True).then_inc(sc_ready, 1)

            def outputs(at, p):
                n, par = NP * at.par + p, at.par
                past(pe, exp_done, at, NP, 0, p + 1)
                if p % 4 == 0:
                    past(pe, raw_out, at, 2, 0, p // 4)
                for h in range(H):
                    gg, hh = h % 4, h // 4
                    c0 = PR * (p % 4) + CH * hh
                    pe.matmul(PVb[32 * gg:32 * gg + 32, c0:c0 + CH], Vz[:, par, p, h].rearrange("p c d -> p (c d)"),
                              PT[:, n % PTS, CH * h:CH * h + CH], start=True, stop=True, tile_position=(0, 32 * gg))
                for gg in range(4):
                    rhs = PT[:, n % PTS, :].rearrange("p (a g q) -> p a g q", a=2, g=4)[:, :, gg, :]
                    ins = pe.matmul(DN[32 * gg:32 * gg + 32, PR * (p % 4):PR * (p % 4) + PR],
                                    onesbd.rearrange("p c d -> p (c d)"), rhs, start=True, stop=True,
                                    tile_position=(0, 32 * gg))
                ins.then_inc(pv_done, 1)

            def tail(at):
                o = (at.par + 1) % 2
                for c in range(2):
                    dst = put(pe, at, f"wo{c}")
                    if c == 0:
                        if at.first(-2):
                            pe.wait_ge(wo_in, 256)
                        past(pe, norm_done, at, NP, 0, 0)
                    for hh in range(2):
                        ins = pe.matmul(dst[:], WOZ[:, 2 * c + hh, :], On[:, o, :, hh, :], start=(hh == 0), stop=(hh == 1))
                    ins.then_inc(ready_sem(at, f"wo{c}"), 1)

            def body(at):
                if at is START:
                    for name in FRONT:
                        front(at, name)
                    for p in range(LEAD):
                        max_scores(At(0, 0), p)
                    return
                if at is None:
                    tail(LAST)
                    return
                more = has_front(at)
                for p in range(NP):
                    scores(at, p)
                    if p + LEAD < NP or more:
                        max_scores(*ahead(at, p))
                    if p:
                        outputs(at, p - 1)
                    if p == TAIL_AT and not at.first(-1):
                        tail(at)
                    if more:
                        for name in PLACE[p]:
                            front(at, name)
                outputs(at, NP - 1)

            batches(pe, body)


def kernel(**inputs):
    import numpy as np
    import concourse.bacc as bacc
    from concourse.bass_utils import run_bass_kernel_spmd

    a = {n: np.asarray(v) for n, v in inputs.items()}
    x, g, mask = a["x"], a["ctx_4096"], a["mask_Bx1x4096_ff1"]
    w = {n[len("L0_xattn_"):]: v for n, v in a.items() if n.startswith("L0_xattn_")}
    b_in = a["L1_xattn_b_in"]

    row = np.arange(C)
    onesbd = (row[:, None] // CH == np.arange(2 * D)[None, :] // D).astype(np.float32)
    stacked = (row[:, None] % CH == np.arange(CH)[None, :]).astype(np.float32)
    off = np.where(row[:, None] // D == row[None, :] // D, 0.0, OFF).astype(np.float32)
    indicator = (np.arange(2)[:, None] == row[None, :] // CH).astype(np.float32)
    b_col = np.stack([b_in[0:C], b_in[C:2 * C], a["L1_xattn_b_out"], np.zeros(C, np.float32)], axis=1)

    arrays = {
        "x_in": x, "g_in": g, "xT_in": x.transpose(0, 2, 1), "gT_in": g.transpose(0, 2, 1), "mask_in": mask,
        "mask_ck_in": mask.reshape(B, NP, PR).transpose(2, 0, 1).reshape(PR, B * NP),
        "w_first_in": np.concatenate([a["L1_xattn_W_in"].T, onesbd, stacked, b_col], axis=1),
        "w_second_in": np.concatenate([w["wq_rgb"].T, w["wk_rgb"].T, w["wk_point"].T, w["wq_point"].T,
                                       w["proj_p2r"].T, w["proj_r2p"].T, w["wv_point"], w["wv_rgb"],
                                       np.eye(C, dtype=np.float32), off], axis=1),
        "wo_in": a["L1_xattn_W_out"].T, "b_v_in": b_in[2 * C:3 * C].reshape(1, C), "indicator_in": indicator,
    }
    arrays = {n: np.ascontiguousarray(v) for n, v in arrays.items()}
    nc = bacc.Bacc("TRN2", target_bir_lowering=False, num_devices=1)
    args = [nc.dram_tensor(n, v.shape, mybir.dt.from_np(v.dtype), kind="ExternalInput").ap() for n, v in arrays.items()]
    args.append(nc.dram_tensor("y_out", (B, C, T), F32, kind="ExternalOutput").ap())
    program(nc, *args)
    r = run_bass_kernel_spmd(nc, [arrays], core_ids=[0])
    return r.results[0]["y_out"]
```

```python
from contextlib import ExitStack

import concourse.bass as bass
from concourse import mybir

B, C, T, H = 16, 128, 1024, 8
D = C // H
CH = 64
PR = 2 * CH
NP = T // PR
HALF = T // 2
SCALE = float(D) ** -0.5
NEG = -998244352.0
PTS = 2
LEAD = 2
OFF = -1.0e30
EPS = 1e-5

F32 = mybir.dt.float32
F32R = mybir.dt.float32r
BF16 = mybir.dt.bfloat16
ALU = mybir.AluOpType
ACT = mybir.ActivationFunctionType
AX_X = mybir.AxisListType.X

ORDER = ["k0", "V0", "k1", "q0", "M", "q1", "A", "S", "V1", "QA", "PM", "wo0", "wo1", "y0", "y1"]
TAIL = ["wo0", "wo1"]
FRONT = [name for name in ORDER if name not in TAIL]
START_FRONT = ["k0", "k1", "q0", "M", "q1", "A", "V0", "S", "V1", "QA", "PM", "y0", "y1"]
PLACE = {0: [], 1: ["k0", "V0", "k1"], 2: ["q0", "M", "q1", "A"], 3: ["S", "V1"], 4: ["QA"], 5: ["PM"], 6: [],
         7: ["y0", "y1"]}
TURN_AT = 3
TAIL_AT = (5, 6)
USES = len(ORDER)
FIRST = 3 * C + 2 * D + CH + 4


def program(nc, x, g, xT, gT, mask, mask_ck, w_first, w_second, wo, wo_split, b_v, indicator, out):
    with ExitStack() as ctx:
        def sb(name, shape, dt=F32):
            return ctx.enter_context(nc.sbuf_tensor(name, shape, dt))

        def sb_over(names, shape):
            with nc.sbuf_tensor(names[0], [C, T], F32) as t:
                pass
            return t, sb(names[1], shape, F32R)

        def ps(name):
            return ctx.enter_context(nc.psum_tensor(name, [C, HALF], F32))

        def sem(name):
            return ctx.enter_context(nc.semaphore(name))

        G, Gh, Gl = sb("G", [C, T]), sb("Gh", [C, T], F32R), sb("Gl", [C, T], F32R)
        X = sb("X", [C, T])
        XT, Odh = sb_over(["XT", "Odh"], [C, 2, 2, NP // 2, CH])
        GT, Odl = sb_over(["GT", "Odl"], [C, 2, 2, NP // 2, CH])
        mrow = sb("mrow", [2, NP, CH])
        first = sb("first", [C, FIRST])
        WQKV = first[:, 0:3 * C].rearrange("p (a c) -> p a c", c=C)
        onesbd = first[:, 3 * C:3 * C + 2 * D].rearrange("p (c d) -> p c d", c=2)
        Wh, Wl = sb("Wh", [C, 2, C], F32R), sb("Wl", [C, 2, C], F32R)
        bcol = first[:, FIRST - 4:FIRST]
        second = sb("second", [C, 10, C])
        WL0 = second[:, 0:6, :]
        WV = second[:, 6:8, :]
        ident, offb = second[:, 8, :], second[:, 9, :]
        WOh, WOl = sb("WOh", [C, C], F32R), sb("WOl", [C, C], F32R)
        bv = sb("bv", [C, C])
        i2b = sb("i2b", [C, CH], BF16)
        indb = sb("indb", [2, C], BF16)
        nb = sb("nb", [C, B * NP])
        halfneg = sb("halfneg", [C, 1])
        epsc = sb("epsc", [C, 1])
        carrier = sb("carrier", [C, 1])
        Msb = sb("Msb", [C, C])
        Asb = sb("Asb", [C, 2, C])
        Ssb = sb("Ssb", [C, 2, C])
        nmx0 = sb("nmx0", [C, 2])
        E0 = Ssb
        sum0 = sb("sum0", [C, 2])
        rs0 = sb("rs0", [C, 2])
        ET = sb("ET", [C, 2, C])
        QAsb = Asb
        WYG, WYX = sb("WYG", [C, C]), sb("WYX", [C, C])
        WYh, WYl = sb("WYh", [C, C], F32R), sb("WYl", [C, C], F32R)
        Y = sb("Y", [C, 2, T])
        qs = sb("qs", [C, T])
        qb = sb("qb", [C, 2, T], BF16)
        ks = sb("ks", [C, 2, T])
        kb = sb("kb", [C, T], BF16)
        Qz0, Qz1 = sb("Qz0", [C, H, T]), sb("Qz1", [C, H, T])
        Kz0, Kz1 = sb("Kz0", [C, H, T], BF16), sb("Kz1", [C, H, T], BF16)
        Qz, Kz = [Qz0, Qz1], [Kz0, Kz1]
        Vz = sb("Vz", [C, 2, NP, H, 2, D])
        mbias = sb("mbias", [2, 2, NP, CH], BF16)
        nmx = sb("nmx", [C, 2, H], BF16)
        mex = sb("mex", [C, 2, H, CH], BF16)
        bones = sb("bones", [C, 2, CH], BF16)
        PT = sb("PT", [C, PTS, HALF])
        den = sb("den", [C, HALF])
        On = sb("On", [C, 2, 2, NP // 2, CH])
        Od = sb("Od", [C, 2, 2, NP // 2, CH])
        R = sb("R", [C, T])
        maskb = sb("maskb", [C, T])
        stats = sb("stats", [C, 2, 6])
        mv = sb("mv", [C, 2])
        ve = sb("ve", [C, 1])
        rstd = sb("rstd", [C, 1])

        misc = [ps("misc0"), ps("misc1")]
        MX = [ps("mx0"), ps("mx1")]
        SC = [ps("sc0"), ps("sc1")]
        PVb, DN = ps("pv"), ps("dn")

        first_in = sem("first_in")
        consts_in = sem("consts_in")
        wo_in = sem("wo_in")
        setup = sem("setup")
        setup_pool = sem("setup_pool")
        setup_act = sem("setup_act")
        zeroed_pool, zeroed_dve = sem("zeroed_pool"), sem("zeroed_dve")
        maskb_in = sem("maskb_in")
        x_in, g_in, turned_in = sem("x_in"), sem("g_in"), sem("turned_in")
        g_high, g_split = sem("g_high"), sem("g_split")
        wy_high, wy_split = sem("wy_high"), sem("wy_split")
        misc_ready = [sem("misc_ready0"), sem("misc_ready1")]
        misc_out = [sem("misc_out0"), sem("misc_out1")]
        l0_max, l0_exp, l0_turned = sem("l0_max"), sem("l0_exp"), sem("l0_turned")
        cast_k, cast_q = sem("cast_k"), sem("cast_q")
        q_spread = [sem("q_spread0"), sem("q_spread1")]
        k_spread = [sem("k_spread0"), sem("k_spread1")]
        mbias_ready = sem("mbias_ready")
        mx_ready, mx_taken, m_ready = sem("mx_ready"), sem("mx_taken"), sem("m_ready")
        sc_ready, exp_done = sem("sc_ready"), sem("exp_done")
        pv_done = sem("pv_done")
        den_out, raw_out = sem("den_out"), sem("raw_out")
        rden_done, norm_done = sem("rden_done"), sem("norm_done")
        wo_high, wo_rest = sem("wo_high"), sem("wo_rest")
        od_high, od_split = sem("od_high"), sem("od_split")
        kept = sem("kept")
        moved = [sem("moved0"), sem("moved1")]
        last_wo_in = sem("last_wo_in")
        added = sem("added")
        stats_done, aggr_done, ve_done, rstd_done = sem("stats_done"), sem("aggr_done"), sem("ve_done"), sem("rstd_done")
        normed = sem("normed")
        stored = sem("stored")

        class At:
            def __init__(self, i, par):
                self.i, self.par = i, par

            def b(self, shift=0):
                return self.i * 2 + (self.par + shift)

            def first(self, shift=0):
                return isinstance(self.i, int) and self.b(shift) < 0

        def past(eng, s, at, per, shift, extra):
            if isinstance(at.i, int) and per * at.b(shift) + extra <= 0:
                return
            eng.wait_ge(s, at.i * (2 * per) + (per * (at.par + shift) + extra))

        def use(at, name):
            front, tail, base = len(FRONT), len(TAIL), 0
            if at is None:
                n = START_FRONT.index(name)
            elif not isinstance(at.i, int):
                n, base = 2 * front - USES + USES * at.par + ORDER.index(name), at.i * USES
            elif at.b() == 0:
                n = front + FRONT.index(name)
            else:
                n = 2 * front + USES * (at.b() - 1)
                if at.b() >= B - 1:
                    n += TAIL.index(name) - (front if at.b() == B else 0)
                else:
                    n += ORDER.index(name)
            return n % 2, n // 2, base

        def wait_use(eng, sems, at, name, back):
            bank, turn, base = use(at, name)
            if isinstance(base, int) and base + turn + back <= 0:
                return
            eng.wait_ge(sems[bank], base + (turn + back))

        def take(eng, at, name):
            wait_use(eng, misc_ready, at, name, 1)
            return misc[use(at, name)[0]]

        def put(eng, at, name):
            wait_use(eng, misc_out, at, name, 0)
            return misc[use(at, name)[0]]

        def evicted(eng, at, name):
            wait_use(eng, misc_out, at, name, 1)

        def out_sem(at, name):
            return misc_out[use(at, name)[0]]

        def ready_sem(at, name):
            return misc_ready[use(at, name)[0]]

        def flat(outputs, j):
            return outputs[:, j].rearrange("p a n q -> p (a n q)")

        def pairs(t, start, end):
            return t[:].rearrange("p (a n q) -> p a n q", a=2, q=CH)[:, :, start:end]

        START = At(-1, 1)

        def fr(at):
            return None if at is START else at

        def nxt(at):
            return (at.par + 1) % 2

        def batches(eng, body):
            body(START)
            body(At(0, 0))
            body(At(0, 1))
            with eng.Fori(1, B // 2 - 1) as i:
                body(At(i, 0))
                body(At(i, 1))
            body(At(B // 2 - 1, 0))
            body(At(B // 2 - 1, 1))
            body(None)

        def has_front(at):
            return at is START or not (isinstance(at.i, int) and at.b() == B - 1)

        def is_last(at):
            return isinstance(at.i, int) and at.b() == B - 1

        def following(at):
            return At(at.i, 1) if at.par == 0 else At(at.i + 1, 0)

        def ahead(at, p):
            return (at, p + LEAD) if p + LEAD < NP else (following(at), p + LEAD - NP)

        last_wo, last_R = X[:, 0:4 * C], G[:]

        WO = R[:, 0:C]

        LAST = At(B // 2, 0)

        def wait_spread(eng, sems, at):
            eng.wait_ge(sems[at.par], at.i * (16 * H) + 16 * H)

        def before(at):
            if isinstance(at.i, int) and at.b() == 0:
                return START
            return At(at.i, 0) if at.par == 1 else At(at.i + (-1), 1)

        def as32(t):
            return t.bitcast(F32)

        def split_g(eng, at, j):
            past(eng, g_high, at, 1, 1, 1)
            cols = slice(HALF * j, HALF * j + HALF)
            eng.tensor_tensor(Gl[:, cols], G[:, cols], as32(Gh[:, cols]), ALU.subtract).then_inc(g_split, 1)

        block = ctx.enter_context(nc.Block())

        @block.sync
        def _(sp):
            def load_g(b):
                sp.dma_start(G[:], g[b]).then_inc(g_in, 16)

            def load_x(b):
                sp.dma_start(X[:], x[b]).then_inc(x_in, 16)

            def load_turned(b):
                for dst, src in ((XT, xT), (GT, gT)):
                    sp.dma_start(dst[:], src[b].rearrange("(p t) c -> p (t c)", t=T // C)).then_inc(turned_in, 16)
                sp.dma_start(mrow[:], mask[b].rearrange("o (p c k) -> (o c) p k", c=2, k=CH)).then_inc(turned_in, 16)

            def load_mask(b):
                sp.dma_start(maskb[:], mask[b].to_broadcast([C, T])).then_inc(maskb_in, 16)

            sp.dma_start(first[:], w_first).then_inc(first_in, 16)
            load_g(0)
            sp.dma_start(Msb[0:2, :], indicator).then_inc(first_in, 16)
            sp.dma_start(bv[:], b_v.to_broadcast([C, C])).then_inc(first_in, 16)
            load_turned(0)
            sp.dma_start(second[:], w_second.rearrange("p (a c) -> p a c", c=C)).then_inc(consts_in, 16)
            sp.dma_start(nb[:], mask_ck).then_inc(consts_in, 16)
            load_x(0)

            def move(j):
                for gg in range(4):
                    lo, hi = slice(32 * gg, 32 * gg + D), slice(32 * gg + D, 32 * gg + 2 * D)
                    sp.dma_start(Od[hi, j, 0], On[lo, j, 1]).then_inc(moved[j], 16)
                    sp.dma_start(Od[lo, j, 1], On[hi, j, 0]).then_inc(moved[j], 16)

            def body(at):
                if at is None:
                    at = LAST
                n = nxt(at)
                if isinstance(at.i, int) and at.b() == 0:
                    sp.dma_start(WO, wo).then_inc(wo_in, 16)
                    load_mask(0)
                moves = at is not START and at is not LAST and not at.first(-1)
                if moves:
                    past(sp, kept, at, 2, -1, 1)
                    move(0)
                more = not (at is LAST or isinstance(at.i, int) and at.b(2) >= B)
                if at is not START and at is not LAST and has_front(at):
                    wait_use(sp, misc_ready, fr(before(at)), "y1", 1)
                    load_x(at.b(1))
                if at is START:
                    sp.wait_ge(zeroed_dve, 1)
                elif at.first(-1):
                    sp.wait_ge(zeroed_pool, 3)
                if at is not LAST and has_front(at):
                    past(sp, cast_k, at, 2, 1, 2)
                    for h in range(H):
                        sp.dma_start(Kz[n][D * h:D * h + D, h, :], kb[D * h:D * h + D, :]).then_inc(k_spread[n], 16)
                if moves:
                    past(sp, kept, at, 2, -1, 2)
                    move(1)
                    if is_last(at):
                        sp.dma_start(last_wo, wo_split).then_inc(last_wo_in, 16)
                if at is not LAST and has_front(at):
                    if at is START:
                        sp.wait_ge(zeroed_pool, 1)
                    evicted(sp, fr(at), "q1")
                    for h in range(H):
                        sp.dma_start(Qz[n][D * h:D * h + D, h, :], qs[D * h:D * h + D, :]).then_inc(q_spread[n], 16)
                if more:
                    if at is START or at.first(-1):
                        evicted(sp, fr(at), "S")
                        load_turned(at.b(2))
                    if at is START:
                        sp.wait_ge(g_split, 2)
                    wait_use(sp, misc_ready, fr(at), "V1", 1)
                    load_g(at.b(2))
                if at is not START and not at.first(-1):
                    if at is not LAST:
                        evicted(sp, at, "wo1")
                        load_mask(at.b())
                    if more:
                        load_turned(at.b(2))
                    past(sp, normed, at, 1, -1, 1)
                    sp.dma_start(out[at.b(-1)], last_R if at is LAST else R[:]).then_inc(stored, 16)
            batches(sp, body)
            sp.wait_ge(stored, 16 * B)

        @block.gpsimd
        def _(pool):
            pool.memset(Vz[:, 1], 0.0).then_inc(setup_pool, 1)
            pool.memset(halfneg[:], -0.5).then_inc(setup_pool, 1)
            pool.memset(epsc[:], EPS).then_inc(setup_pool, 1)
            pool.memset(Qz0[:], 0.0).then_inc(zeroed_pool, 1)
            pool.memset(Kz1[:].bitcast(F32), 0.0).then_inc(zeroed_pool, 1)
            pool.memset(Qz1[:], 0.0).then_inc(zeroed_pool, 1)
            pool.wait_ge(setup_pool, 3)
            pool.wait_ge(setup, 3)

            def spread_max(at, p):
                n = NP * at.par + p
                past(pool, mx_taken, at, NP, 0, p + 1)
                past(pool, sc_ready, at, NP, 0, p - 1)
                nc.gpsimd.tensor_tensor(mex[:, n % 2], nmx[:, n % 2, :, None].to_broadcast([C, H, CH]),
                                        i2b[:, None, :].to_broadcast([C, H, CH]), ALU.mult).then_inc(m_ready, 1)

            def tail(at, j):
                evicted(pool, at, f"wo{j}")
                r = R[:, HALF * j:HALF * j + HALF]
                nc.gpsimd.tensor_tensor(r, r, Y[:, nxt(at), HALF * j:HALF * j + HALF], ALU.add).then_inc(added, 1)

            def split_od(at, j):
                past(pool, od_high, at, 2, -1, j + 1)
                nc.gpsimd.tensor_tensor(flat(Odl, j), flat(Od, j), as32(flat(Odh, j)), ALU.subtract).then_inc(od_split, 1)

            def root(at):
                past(pool, aggr_done, at, 1, 0, 0)
                nc.gpsimd.tensor_tensor(ve[:], mv[:, 1:2], epsc[:], ALU.add).then_inc(ve_done, 1)
                past(pool, ve_done, at, 1, 0, 0)
                nc.gpsimd.tensor_tensor(rstd[:], ve[:], halfneg[:], ALU.pow).then_inc(rstd_done, 1)

            def body(at):
                if at is START:
                    for p in range(LEAD):
                        spread_max(At(0, 0), p)
                    split_g(pool, following(at), 0)
                    return
                if at is None:
                    root(LAST)
                    return
                more = has_front(at)
                for p in range(NP):
                    if p == 0 and more:
                        split_g(pool, at, 1)
                    if p + LEAD < NP or more:
                        spread_max(*ahead(at, p))
                    if p in (3, 5) and not at.first(-1):
                        split_od(at, p // 5)
                    if p - 1 in TAIL_AT and not at.first(-1):
                        tail(at, p - 1 - TAIL_AT[0])
                    if p == NP - 1 and more and has_front(following(at)):
                        split_g(pool, following(at), 0)
                    if p == NP - 1 and not at.first(-1):
                        root(at)

            batches(pool, body)

        @block.scalar
        def _(act):
            act.wait_ge(first_in, 48)
            nc.scalar.mul(bcol[:, 3:4], bcol[:, 0:1], SCALE).then_inc(setup_act, 1)
            act.wait_ge(setup, 3)
            act.wait_ge(setup_act, 1)

            def front(at, name):
                n, a = nxt(at), fr(at)
                if name == "M":
                    src = take(act, a, name)
                    nc.scalar.copy(Msb[:], src[:, 0:C]).then_inc(out_sem(a, name), 1)
                if name == "A":
                    src = take(act, a, name)
                    nc.scalar.copy(Asb[:], src[:, 0:2 * C].rearrange("p (a c) -> p a c", a=2)).then_inc(out_sem(a, name), 1)
                if name == "S":
                    past(act, l0_max, at, 1, 1, 1)
                    for d in range(2):
                        nc.scalar.activation(E0[:, d, :], Ssb[:, d, :], ACT.Exp, bias=nmx0[:, d:d + 1],
                                             accum_out=sum0[:, d:d + 1]).then_inc(l0_exp, 1)
                if name == "QA":
                    src = take(act, a, name)
                    past(act, l0_turned, at, 2, 1, 2)
                    for d in range(2):
                        ins = nc.scalar.mul(QAsb[:, d, :], src[:, d * C:d * C + C], rs0[:, d:d + 1])
                    ins.then_inc(out_sem(a, name), 1)
                if name in ("y0", "y1"):
                    j = int(name[1])
                    src = take(act, a, name)
                    if j == 0:
                        past(act, added, at, 2, 0, 0)
                    nc.scalar.copy(Y[:, n, HALF * j:HALF * j + HALF], src[:]).then_inc(out_sem(a, name), 1)
                if name in ("q0", "q1"):
                    j = int(name[1])
                    src = take(act, a, name)
                    if j == 0:
                        past(act, mx_ready, at, NP, 0, 0)
                        past(act, sc_ready, at, NP, 0, 0)
                        if at is not START:
                            wait_spread(act, q_spread, at)
                    cols = slice(HALF * j, HALF * j + HALF)
                    nc.scalar.activation(qs[:, cols], src[:], ACT.Identity, bias=bcol[:, 3:4],
                                         scale=SCALE).then_inc(out_sem(a, name), 1)
                    evicted(act, a, name)
                    nc.scalar.copy(qb[:, n, cols], qs[:, cols]).then_inc(cast_q, 1)
                if name in ("k0", "k1"):
                    j = int(name[1])
                    src = take(act, a, name)
                    if j == 0:
                        past(act, sc_ready, at, NP, 0, 0)
                        past(act, mx_ready, at, NP, 0, 0)
                        if at is not START:
                            wait_spread(act, k_spread, at)
                    cols = slice(HALF * j, HALF * j + HALF)
                    nc.scalar.activation(ks[:, n, cols], src[:], ACT.Identity,
                                         bias=bcol[:, 1:2]).then_inc(out_sem(a, name), 1)
                    evicted(act, a, name)
                    nc.scalar.copy(kb[:, cols], ks[:, n, cols]).then_inc(cast_k, 1)

            def body(at):
                if at is None:
                    return
                if at is START:
                    for name in START_FRONT:
                        front(at, name)
                    return
                for p in range(NP):
                    past(act, sc_ready, at, NP, 0, p + 1)
                    past(act, pv_done, at, NP, 0, p - 1)
                    exp_pair(at, p)
                    if p == 4:
                        sums(at, 0, 0, 4)
                    if p == 6 and is_last(at):
                        sums(at, 1, 0, 2)
                    if p == 0 and not at.first(-1):
                        keep(at, 0)
                    if has_front(at):
                        for name in PLACE[p]:
                            front(at, name)
                            if name == "M" and not at.first(-1):
                                keep(at, 1)
                    elif p == 2:
                        keep(at, 1)
                sums(at, 1, 2 if is_last(at) else 0, 4)

            def keep(at, j):
                past(act, norm_done, at, NP, -1, 4 * j + 4)
                nc.scalar.copy(flat(Od, j), flat(On, j)).then_inc(kept, 1)

            def sums(at, j, start, end):
                past(act, pv_done, at, NP, 0, 4 * j + end)
                past(act, norm_done, at, NP, 0, 4 * j - 4 + end)
                nc.scalar.copy(pairs(den, start, end), pairs(DN, start, end)).then_inc(den_out, 1)
                past(act, moved[j], at, 16 * 8, 0, 0)
                nc.scalar.copy(On[:, j, :, start:end], pairs(PVb, start, end)).then_inc(raw_out, 1)

            def exp_pair(at, p):
                n = NP * at.par + p
                col = nb[:, bass.ds(at.i * (2 * NP) + n, 1)] if not isinstance(at.i, int) else nb[:, 2 * NP * at.i + n:2 * NP * at.i + n + 1]
                nc.scalar.activation(PT[:, n % PTS, :], SC[n % 2][:], ACT.Exp, bias=col).then_inc(exp_done, 1)

            batches(act, body)

        @block.vector
        def _(dve):
            dve.memset(Kz0[:].bitcast(F32), 0.0).then_inc(zeroed_dve, 1)
            dve.memset(Vz[:, 0], 0.0).then_inc(zeroed_dve, 1)
            dve.wait_ge(first_in, 48)
            dve.tensor_copy(i2b[:], first[:, FIRST - 4 - CH:FIRST - 4]).then_inc(setup, 1)
            dve.tensor_copy(bones[:], onesbd[:, :, 0:1].to_broadcast([C, 2, CH])).then_inc(setup, 1)
            dve.tensor_copy(indb[:], Msb[0:2, :]).then_inc(setup, 1)
            dve.tensor_copy(Wh[:], WQKV[:, 0:2, :]).then_inc(setup, 1)
            dve.wait_ge(setup, 4)
            dve.tensor_tensor(Wl[:], WQKV[:, 0:2, :], as32(Wh[:]), ALU.subtract).then_inc(setup, 1)
            dve.wait_ge(consts_in, 32)
            dve.tensor_scalar(nb[:], nb[:], 0.0, NEG, ALU.is_le, ALU.mult).then_inc(setup, 1)
            dve.wait_ge(setup, 6)
            dve.wait_ge(setup_pool, 3)

            def masked(at, dst, *halves):
                for j in halves:
                    src = take(dve, at, f"wo{j}")
                    if j == 0:
                        past(dve, maskb_in, at, 16, 0, 0)
                    for c in range(2):
                        m, r = (t.rearrange("p (j n c k) -> p j c n k", j=2, c=2, k=CH)[:, j, c] for t in (maskb[:], dst))
                        ins = nc.vector.scalar_tensor_tensor(
                            out=r, in0=src[:].rearrange("p (c n k) -> p c n k", c=2, k=CH)[:, c],
                            scalar=bcol[:, 2:3], in1=m, op0=ALU.add, op1=ALU.mult)
                    ins.then_inc(out_sem(at, f"wo{j}"), 1)
                    if at is LAST:
                        evicted(dve, at, f"wo{j}")
                        cols = slice(HALF * j, HALF * j + HALF)
                        nc.vector.tensor_tensor(dst[:, cols], dst[:, cols], Y[:, nxt(at), cols], ALU.add).then_inc(added, 1)
                        dve.wait_ge(added, 2 * (B - 1) + j + 1)
                        nc.vector.bn_stats(stats[:, j, :], dst[:, cols]).then_inc(stats_done, 1)

            def tail(at, j):
                if j == 0:
                    past(dve, stored, at, 16, -1, 0)
                masked(at, R[:], j)

            def norm(at):
                if at is not LAST:
                    past(dve, added, at, 2, 0, 0)
                    for j in range(2):
                        nc.vector.bn_stats(stats[:, j, :], R[:, HALF * j:HALF * j + HALF]).then_inc(stats_done, 1)
                past(dve, stats_done, at, 2, 0, 0)
                nc.vector.memset(carrier[:], 0.0)
                nc.vector.bn_aggr(mv[:], stats[:].rearrange("p a s -> p (a s)")).then_inc(aggr_done, 1)

            def scale_out(at):
                past(dve, rstd_done, at, 1, 0, 0)
                r = last_R if at is LAST else R[:]
                nc.vector.tensor_scalar(r, r, mv[:, 0:1], rstd[:, 0:1], ALU.subtract,
                                        ALU.mult).then_inc(normed, 1)

            def mask_rows(at):
                past(dve, turned_in, at, 48, 1, 48)
                past(dve, mx_ready, at, NP, 0, 0)
                nc.vector.tensor_scalar(mbias[:, nxt(at)], mrow[:], 0.0, NEG, ALU.is_le,
                                        ALU.mult).then_inc(mbias_ready, 1)

            def front(at, name):
                n, a = nxt(at), fr(at)
                if name == "S":
                    src = take(dve, a, name)
                    nc.vector.scalar_tensor_tensor(
                        out=Ssb[:], in0=src[:, 0:2 * C].rearrange("p (a c) -> p a c", a=2), scalar=SCALE,
                        in1=offb[:, None, :].to_broadcast([C, 2, C]), op0=ALU.mult, op1=ALU.add).then_inc(out_sem(a, name), 1)
                    evicted(dve, a, name)
                    nc.vector.tensor_reduce(nmx0[:], Ssb[:], AX_X, ALU.max, negate=True).then_inc(l0_max, 1)
                if name == "turn":
                    past(dve, l0_exp, at, 2, 1, 2)
                    nc.vector.reciprocal(rs0[:], sum0[:]).then_inc(l0_turned, 1)
                    nc.vector.transpose(ET[:].rearrange("p a c -> p (a c)"), E0[:].rearrange("p a c -> p (a c)")).then_inc(l0_turned, 1)
                if name == "PM":
                    src = take(dve, a, name)
                    for w, dst in enumerate((WYG, WYX)):
                        ins = nc.vector.tensor_tensor(dst[:], src[:, C * w:C * w + C], ident, ALU.add)
                    ins.then_inc(out_sem(a, name), 1)
                    evicted(dve, a, name)
                    nc.vector.tensor_copy(WYh[:], WYG[:]).then_inc(wy_high, 1)
                    past(dve, wy_high, at, 1, 1, 1)
                    nc.vector.tensor_tensor(WYl[:], WYG[:], as32(WYh[:]), ALU.subtract).then_inc(wy_split, 1)
                if name in ("V0", "V1"):
                    j = int(name[1])
                    src = take(dve, a, name)
                    past(dve, pv_done, at, NP, 0, 0)
                    for c in range(2):
                        rows = slice(CH * c, CH * c + CH)
                        o = Vz[rows, n, 4 * j:4 * j + 4, :, c, :]
                        s = src[rows, :].rearrange("p (n h d) -> p n h d", n=4, d=D)
                        bias = bv[rows, :].rearrange("p (h d) -> p h d", d=D)[:, None].to_broadcast([CH, 4, H, D])
                        ins = nc.vector.tensor_tensor(o, s, bias, ALU.add)
                    ins.then_inc(out_sem(a, name), 1)

            def maxima(at, p):
                n = NP * at.par + p
                past(dve, mx_ready, at, NP, 0, p + 1)
                past(dve, m_ready, at, NP, 0, p - 1)
                nc.vector.tensor_reduce(nmx[:, n % 2, :], MX[n % 2][:].rearrange("p (h k) -> p h k", h=H), AX_X,
                                        ALU.max, negate=True).then_inc(mx_taken, 1)

            def normalise(at, j):
                half, part = j // 4, j % 4
                d = pairs(den, part, part + 1)[:, :, 0]
                split = half == 1 and is_last(at)
                if part == 0 or split and part == 2:
                    past(dve, den_out, at, 2, 0, half + 1 + part // 2)
                nc.vector.reciprocal(d, d).then_inc(rden_done, 1)
                if part == 0 or split and part == 2:
                    past(dve, raw_out, at, 2, 0, half + 1 + part // 2)
                past(dve, rden_done, at, NP, 0, j + 1)
                o = On[:, half, :, part]
                nc.vector.tensor_tensor(o, o, d, ALU.mult).then_inc(norm_done, 1)

            def high_od(at, j):
                if j == 0 and has_front(at):
                    take(dve, at, "M")
                past(dve, moved[j], at, 16 * 8, 0, 0)
                nc.vector.tensor_copy(flat(Odh, j), flat(Od, j)).then_inc(od_high, 1)

            def high_g(at):
                past(dve, g_in, at, 16, 1, 16)
                if at is not START:
                    wait_use(dve, misc_ready, fr(before(at)), "y1", 1)
                nc.vector.tensor_copy(Gh[:], G[:]).then_inc(g_high, 1)

            def body(at):
                if at is START:
                    high_g(at)
                    split_g(dve, at, 0)
                    split_g(dve, at, 1)
                    mask_rows(at)
                    for name in START_FRONT:
                        if name == "QA":
                            front(at, "turn")
                            for p in range(LEAD):
                                maxima(At(0, 0), p)
                        front(at, name)
                    high_g(following(at))
                    return
                if at is None:
                    for j in range(6, NP):
                        normalise(before(LAST), j)
                    scale_out(before(LAST))
                    masked(LAST, last_R, 0, 1)
                    norm(LAST)
                    scale_out(LAST)
                    return
                more = has_front(at)
                for p in range(NP):
                    if p + LEAD < NP or more:
                        maxima(*ahead(at, p))
                    if p == 2 and more:
                        mask_rows(at)
                    if p in (3, 5) and not at.first(-1):
                        high_od(at, p // 5)
                    if p == TAIL_AT[0] and more:
                        front(at, "PM")
                    if p in TAIL_AT and not at.first(-1):
                        tail(at, p - TAIL_AT[0])
                    if p >= 4:
                        normalise(at, p - 4)
                    elif p == 0 and not at.first(-1):
                        normalise(before(at), 4)
                        normalise(before(at), 5)
                    if more and p != TAIL_AT[0]:
                        for name in PLACE[p] + (["turn"] if p == TURN_AT else []):
                            front(at, name)
                    if p == 6 and isinstance(at.i, int) and at.b() == 0:
                        dve.wait_ge(wo_in, 16)
                        nc.vector.tensor_copy(WOh[:], WO).then_inc(wo_high, 1)
                        dve.wait_ge(wo_high, 1)
                        nc.vector.tensor_tensor(WOl[:], WO, as32(WOh[:]), ALU.subtract).then_inc(wo_rest, 1)
                    if p == 1 and not at.first(-1):
                        normalise(before(at), 6)
                        normalise(before(at), 7)
                    if p == NP - 1:
                        if more and has_front(following(at)):
                            high_g(following(at))
                        if not at.first(-1) and not is_last(at):
                            norm(at)
                            scale_out(at)
                        if is_last(at):
                            normalise(at, 4)
                            normalise(at, 5)
                            norm(at)

            batches(dve, body)

        @block.tensor
        def _(pe):
            pe.wait_ge(first_in, 48)

            def product(dst, wh, wl, th, tl, stop=True):
                pe.matmul(dst[:], wh, th, start=True, stop=False)
                pe.matmul(dst[:], wh, tl, start=False, stop=False)
                return pe.matmul(dst[:], wl, th, start=False, stop=stop)

            def front(at, name):
                n, a = nxt(at), fr(at)
                if name == "M":
                    past(pe, turned_in, at, 48, 1, 48)
                if at is START and name == "k0":
                    pe.wait_ge(g_in, 16)
                if at is not START and name in ("k0", "k1"):
                    past(pe, g_split, at, 2, 1, int(name[1]) + 1)
                dst = put(pe, a, name)
                if name == "M":
                    for t in range(T // C):
                        ins = pe.matmul(dst[:, 0:C], XT[:, C * t:C * t + C], GT[:, C * t:C * t + C],
                                        start=(t == 0), stop=(t == T // C - 1))
                if name == "A":
                    evicted(pe, a, "M")
                    if at is START:
                        pe.wait_ge(consts_in, 32)
                    ins = pe.matmul(dst[:, 0:2 * C], Msb[:], WL0[:, 0:2, :], start=True, stop=True)
                if name == "S":
                    evicted(pe, a, "A")
                    pe.matmul(dst[:, 0:C], Asb[:, 0, :], WL0[:, 2, :], start=True, stop=True)
                    ins = pe.matmul(dst[:, C:2 * C], WL0[:, 3, :], Asb[:, 1, :], start=True, stop=True)
                if name == "QA":
                    past(pe, l0_turned, at, 2, 1, 2)
                    pe.matmul(dst[:, 0:C], ET[:, 0, :], WL0[:, 4, :], start=True, stop=True)
                    ins = pe.matmul(dst[:, C:2 * C], ET[:, 1, :], WL0[:, 5, :], start=True, stop=True)
                if name == "PM":
                    evicted(pe, a, "QA")
                    pe.matmul(dst[:, 0:C], WV[:, 0, :], QAsb[:, 0, :], start=True, stop=True)
                    ins = pe.matmul(dst[:, C:2 * C], WV[:, 1, :], QAsb[:, 1, :], start=True, stop=True)
                if name in ("y0", "y1"):
                    if at is START:
                        pe.wait_ge(g_split, 2)
                    past(pe, x_in, at, 16, 1, 16)
                    past(pe, wy_split, at, 1, 1, 1)
                    cols = slice(HALF * int(name[1]), HALF * int(name[1]) + HALF)
                    product(dst, WYh[:], WYl[:], Gh[:, cols], Gl[:, cols], stop=False)
                    ins = pe.matmul(dst[:], WYX[:], X[:, cols], start=False, stop=True)
                if name in ("q0", "q1", "k0", "k1"):
                    w = 0 if name[0] == "q" else 1
                    cols = slice(HALF * int(name[1]), HALF * int(name[1]) + HALF)
                    if at is START:
                        ins = pe.matmul(dst[:], WQKV[:, w], G[:, cols], start=True, stop=True)
                    else:
                        ins = product(dst, Wh[:, w], Wl[:, w], Gh[:, cols], Gl[:, cols])
                if name in ("V0", "V1"):
                    for t in range(4):
                        c0 = HALF * int(name[1]) + C * t
                        ins = pe.matmul(dst[:, C * t:C * t + C], G[:, c0:c0 + C], WQKV[:, 2, :], start=True, stop=True)
                ins.then_inc(ready_sem(a, name), 1)

            def max_scores(at, p):
                n, par = NP * at.par + p, at.par
                if p == 0:
                    wait_spread(pe, k_spread, at)
                    past(pe, cast_q, at, 2, 0, 2)
                    past(pe, mbias_ready, at, 1, 0, 1)
                past(pe, mx_taken, at, NP, 0, p - 1)
                dst = MX[n % 2]
                for c in range(2):
                    cols = slice(PR * p + CH * c, PR * p + CH * c + CH)
                    pe.matmul(dst[CH * c:CH * c + CH, :], qb[:, par, cols], Kz[par][:, :, cols], start=True,
                              stop=False, skip_group_check=True)
                pe.matmul(dst[:], indb[:], mbias[:, par, p, None, :].to_broadcast([2, H, CH]), start=False, stop=True,
                          skip_group_check=True).then_inc(mx_ready, 1)

            def scores(at, p):
                n, par = NP * at.par + p, at.par
                if p == 0:
                    wait_spread(pe, q_spread, at)
                past(pe, exp_done, at, NP, 0, p - 1)
                dst = SC[n % 2]
                for c in range(2):
                    cols = slice(PR * p + CH * c, PR * p + CH * c + CH)
                    pe.matmul(dst[CH * c:CH * c + CH, :], ks[:, par, cols], Qz[par][:, :, cols], start=True,
                              stop=False, skip_group_check=True)
                past(pe, m_ready, at, NP, 0, p + 1)
                pe.matmul(dst[:], bones[:].rearrange("p c k -> p (c k)"), mex[:, n % 2].rearrange("p h q -> p (h q)"),
                          start=False, stop=True, skip_group_check=True).then_inc(sc_ready, 1)

            def outputs(at, p):
                n, par = NP * at.par + p, at.par
                past(pe, exp_done, at, NP, 0, p + 1)
                if p % 4 == 0:
                    past(pe, raw_out, at, 2, 0, p // 4)
                if p == 6 and is_last(at):
                    past(pe, raw_out, at, 2, 0, 2)
                for h in range(H):
                    gg, hh = h % 4, h // 4
                    c0 = HALF // 2 * hh + CH * (p % 4)
                    pe.matmul(PVb[32 * gg:32 * gg + 32, c0:c0 + CH], Vz[:, par, p, h].rearrange("p c d -> p (c d)"),
                              PT[:, n % PTS, CH * h:CH * h + CH], start=True, stop=True, tile_position=(0, 32 * gg))
                for gg in range(4):
                    rhs = PT[:, n % PTS, :].rearrange("p (a g q) -> p a g q", a=2, g=4)[:, :, gg, :]
                    sums = DN[32 * gg:32 * gg + 32, :].rearrange("p (a n q) -> p a n q", a=2, q=CH)[:, :, p % 4]
                    ins = pe.matmul(sums, onesbd.rearrange("p c d -> p (c d)"), rhs, start=True, stop=True,
                                    tile_position=(0, 32 * gg))
                ins.then_inc(pv_done, 1)

            def tail(at, j):
                if isinstance(at.i, int) and at.b() == 1 and j == 0:
                    pe.wait_ge(wo_rest, 1)
                dst = put(pe, at, f"wo{j}")
                past(pe, od_split, at, 2, -1, j + 1)
                product(dst, WOh[:], WOl[:], flat(Odh, j), flat(Odl, j)).then_inc(ready_sem(at, f"wo{j}"), 1)

            def last_tail():
                pe.wait_ge(last_wo_in, 16)
                for j in range(2):
                    dst = put(pe, LAST, f"wo{j}")
                    pe.wait_ge(norm_done, NP * (B - 1) + 4 * j + 4)
                    for c in range(2):
                        cols = slice(HALF // 2 * c, HALF // 2 * c + HALF // 2)
                        for hh in range(2):
                            w = last_wo[:, C * (2 * c + hh):C * (2 * c + hh) + C]
                            ins = pe.matmul(dst[:, cols], w, On[:, j, hh].rearrange("p n q -> p (n q)"),
                                            start=(hh == 0), stop=(hh == 1))
                    ins.then_inc(ready_sem(LAST, f"wo{j}"), 1)

            def body(at):
                if at is START:
                    for name in START_FRONT:
                        if name == "QA":
                            pe.wait_ge(setup, 5)
                            for p in range(LEAD):
                                max_scores(At(0, 0), p)
                        front(at, name)
                    return
                if at is None:
                    last_tail()
                    return
                more = has_front(at)
                for p in range(NP):
                    scores(at, p)
                    if p + LEAD < NP or more:
                        max_scores(*ahead(at, p))
                    if p:
                        outputs(at, p - 1)
                    if more:
                        for name in PLACE[p]:
                            front(at, name)
                    if p in TAIL_AT and not at.first(-1):
                        tail(at, p - TAIL_AT[0])
                outputs(at, NP - 1)

            batches(pe, body)


def kernel(**inputs):
    import numpy as np
    import concourse.bacc as bacc
    from concourse.bass_utils import run_bass_kernel_spmd

    a = {n: np.asarray(v) for n, v in inputs.items()}
    x, g, mask = a["x"], a["ctx_4096"], a["mask_Bx1x4096_ff1"]
    w = {n[len("L0_xattn_"):]: v for n, v in a.items() if n.startswith("L0_xattn_")}
    b_in = a["L1_xattn_b_in"]

    row = np.arange(C)
    onesbd = (row[:, None] // CH == np.arange(2 * D)[None, :] // D).astype(np.float32)
    stacked = (row[:, None] % CH == np.arange(CH)[None, :]).astype(np.float32)
    off = np.where(row[:, None] // D == row[None, :] // D, 0.0, OFF).astype(np.float32)
    indicator = (np.arange(2)[:, None] == row[None, :] // CH).astype(np.float32)
    b_col = np.stack([b_in[0:C], b_in[C:2 * C], a["L1_xattn_b_out"], np.zeros(C, np.float32)], axis=1)

    wo = a["L1_xattn_W_out"].T.reshape(2, 4, D, C)
    wo_split = np.zeros((4, 2, D, 2, 2, C), wo.dtype)
    for c in range(2):
        wo_split[:, c, :, c] = wo.transpose(1, 2, 0, 3)

    arrays = {
        "x_in": x, "g_in": g, "xT_in": x.transpose(0, 2, 1), "gT_in": g.transpose(0, 2, 1), "mask_in": mask,
        "mask_ck_in": mask.reshape(B, NP, PR).transpose(2, 0, 1).reshape(PR, B * NP),
        "w_first_in": np.concatenate([a["L1_xattn_W_in"].T, onesbd, stacked, b_col], axis=1),
        "w_second_in": np.concatenate([w["wq_rgb"].T, w["wk_rgb"].T, w["wk_point"].T, w["wq_point"].T,
                                       w["proj_p2r"].T, w["proj_r2p"].T, w["wv_point"], w["wv_rgb"],
                                       np.eye(C, dtype=np.float32), off], axis=1),
        "wo_in": wo.transpose(1, 0, 2, 3).reshape(C, C), "wo_split_in": wo_split.reshape(C, 4 * C),
        "b_v_in": b_in[2 * C:3 * C].reshape(1, C), "indicator_in": indicator,
    }
    arrays = {n: np.ascontiguousarray(v) for n, v in arrays.items()}
    nc = bacc.Bacc("TRN2", target_bir_lowering=False, num_devices=1)
    args = [nc.dram_tensor(n, v.shape, mybir.dt.from_np(v.dtype), kind="ExternalInput").ap() for n, v in arrays.items()]
    args.append(nc.dram_tensor("y_out", (B, C, T), F32, kind="ExternalOutput").ap())
    program(nc, *args)
    r = run_bass_kernel_spmd(nc, [arrays], core_ids=[0])
    return r.results[0]["y_out"]
```
